# Optimizing a Trainium2 kernel written in Bass

```python
import numpy as np
import jax
import jax.numpy as jnp

def _softmax(x, axis=-1):
    return jax.nn.softmax(x, axis=axis)

def _gelu(x):
    return jax.nn.gelu(x, approximate=True)

def _silu(x):
    return jax.nn.silu(x)

def _sigmoid(x):
    return jax.nn.sigmoid(x)

def _layernorm(x, axis=-1, eps=1e-05):
    m = jnp.mean(x, axis=axis, keepdims=True)
    v = jnp.var(x, axis=axis, keepdims=True)
    return (x - m) / jnp.sqrt(v + eps)

def _scatter_add(tgt, idx, src, axis=0):
    return tgt.at[idx].add(src)

def _segment_sum(src, seg, n):
    return jax.ops.segment_sum(src, seg, n)
kernel_name = 'mk_pixart_resid_d1_seqx_r8_e0ad9f'

def setup_inputs(seed: int=0):
    np.random.seed(seed)
    _w = jnp.asarray

    def _rec_inputs():
        import jax
        import jax.numpy as jnp
        _rk = jax.random.key(seed)
        x = -0.0002928 + 1 * jax.random.normal(jax.random.fold_in(_rk, 1), (64, 64, 128), jnp.float32)
        _lenS = 64 - jax.random.randint(jax.random.fold_in(_rk, 7), (64,), 0, max(1, 64 // 4) + 1, jnp.int32)
        _lenS2 = 64 - jax.random.randint(jax.random.fold_in(_rk, 8), (64,), 0, max(1, 64 // 4) + 1, jnp.int32)
        cond_1024 = 0.000887014 + 1.03683 * jax.random.normal(jax.random.fold_in(_rk, 11), (64, 128), jnp.float32)
        _ctx_1024P = jax.random.normal(jax.random.fold_in(_rk, 12), (64, 16, 128), jnp.float32)
        _ctx_1024c = jax.random.dirichlet(jax.random.fold_in(_rk, 512), 0.3 * jnp.ones((16,), jnp.float32), (64, 64))
        _ctx_1024t = jnp.einsum('bsk,bkd->bsd', _ctx_1024c, _ctx_1024P)
        _ctx_1024t = _ctx_1024t * jax.lax.rsqrt(jnp.mean(jnp.square(_ctx_1024t)) + 1e-12) * 0.953939
        ctx_1024 = -0.000761806 + 0.999296 * (_ctx_1024t + 0.3 * jax.random.normal(jax.random.fold_in(_rk, 612), (64, 64, 128), jnp.float32))
        return (x, cond_1024, ctx_1024)
    x, cond_1024, ctx_1024 = _rec_inputs()

    def _L0_xcond_setup():
        import jax, jax.numpy as jnp
        import numpy as np
        import math
        B, S, CTX, D, H, DH = (2, 256, 32, 128, 16, 64)
        INNER = H * DH
        DFF = 4 * D

        def layernorm(x, eps=1e-05):
            m = jnp.mean(x, axis=-1, keepdims=True)
            v = jnp.var(x, axis=-1, keepdims=True)
            return (x - m) * jax.lax.rsqrt(v + eps)

        def adaln(x, t, w, b):
            emb = t @ w + b
            scale, shift = jnp.split(emb, 2, axis=-1)
            return layernorm(x) * (1.0 + scale) + shift

        def mha(xq, ctx, wq, wk, wv, wo, bo):
            b, sq, _ = xq.shape
            sk = ctx.shape[1]
            q = (xq @ wq).reshape(b, sq, H, DH).transpose(0, 2, 1, 3)
            k = (ctx @ wk).reshape(b, sk, H, DH).transpose(0, 2, 1, 3)
            v = (ctx @ wv).reshape(b, sk, H, DH).transpose(0, 2, 1, 3)
            scores = jnp.einsum('bhqd,bhkd->bhqk', q, k) / math.sqrt(DH)
            attn = jax.nn.softmax(scores, axis=-1)
            out = jnp.einsum('bhqk,bhkd->bhqd', attn, v)
            out = out.transpose(0, 2, 1, 3).reshape(b, sq, INNER)
            return out @ wo + bo

        def glu_ff(x, w1, b1, w2, b2):
            u = x @ w1 + b1
            a, gate = jnp.split(u, 2, axis=-1)
            return a * jax.nn.gelu(gate, approximate=False) @ w2 + b2
        key = jax.random.key(seed)
        ks = jax.random.split(key, 24)
        s = 1.0 / math.sqrt(D)

        def n(k, shape, scale=1.0):
            return jax.random.normal(k, shape, dtype=jnp.float32) * scale
        return {'x': n(ks[0], (B, S, D)), 't': n(ks[1], (B, 1, D)), 'context': n(ks[2], (B, CTX, D)), 'attn1_wq': n(ks[3], (D, INNER), s), 'attn1_wk': n(ks[4], (D, INNER), s), 'attn1_wv': n(ks[5], (D, INNER), s), 'attn1_wo': n(ks[6], (INNER, D), s), 'attn1_bo': n(ks[7], (D,), 0.01), 'attn2_wq': n(ks[8], (D, INNER), s), 'attn2_wk': n(ks[9], (D, INNER), s), 'attn2_wv': n(ks[10], (D, INNER), s), 'attn2_wo': n(ks[11], (INNER, D), s), 'attn2_bo': n(ks[12], (D,), 0.01), 'ff_w1': n(ks[13], (D, 2 * DFF), s), 'ff_b1': n(ks[14], (2 * DFF,), 0.01), 'ff_w2': n(ks[15], (DFF, D), 1.0 / math.sqrt(DFF)), 'ff_b2': n(ks[16], (D,), 0.01), 'norm1_w': n(ks[17], (D, 2 * D), s), 'norm1_b': n(ks[18], (2 * D,), 0.01), 'norm2_w': n(ks[19], (D, 2 * D), s), 'norm2_b': n(ks[20], (2 * D,), 0.01), 'norm3_w': n(ks[21], (D, 2 * D), s), 'norm3_b': n(ks[22], (2 * D,), 0.01)}
    _L0_xcond_all = _L0_xcond_setup()
    _L0_xcond_in = {k: v for k, v in _L0_xcond_all.items() if k in ('attn1_wq', 'attn1_wk', 'attn1_wv', 'attn1_wo', 'attn1_bo', 'attn2_wq', 'attn2_wk', 'attn2_wv', 'attn2_wo', 'attn2_bo', 'ff_w1', 'ff_b1', 'ff_w2', 'ff_b2', 'norm1_w', 'norm1_b', 'norm2_w', 'norm2_b', 'norm3_w', 'norm3_b')}
    del _L0_xcond_all

    def _L0_ffn_setup():
        import jax, jax.numpy as jnp
        import numpy as np
        HIDDEN = 128
        NUM_EXPERTS = 8
        TOP_K = 2
        key = jax.random.key(seed)
        k_x, k_r, k_w1, k_w2 = jax.random.split(key, 4)
        x = jax.random.normal(k_x, (4, 256, HIDDEN), dtype=jnp.float32)
        router_w = jax.random.normal(k_r, (NUM_EXPERTS, HIDDEN), dtype=jnp.float32) * HIDDEN ** (-0.5)
        w1 = jax.random.normal(k_w1, (NUM_EXPERTS, HIDDEN, 2 * HIDDEN), dtype=jnp.float32) * HIDDEN ** (-0.5)
        w2 = jax.random.normal(k_w2, (NUM_EXPERTS, 2 * HIDDEN, HIDDEN), dtype=jnp.float32) * (2 * HIDDEN) ** (-0.5)
        return {'x': x, 'router_w': router_w, 'w1': w1, 'w2': w2}
    _L0_ffn_all = _L0_ffn_setup()
    _L0_ffn_in = {k: v for k, v in _L0_ffn_all.items() if k in ('router_w', 'w1', 'w2')}
    del _L0_ffn_all
    return {'x': x, 'cond_1024': cond_1024, 'ctx_1024': ctx_1024, 'L0_xcond_attn1_wq': _L0_xcond_in['attn1_wq'], 'L0_xcond_attn1_wk': _L0_xcond_in['attn1_wk'], 'L0_xcond_attn1_wv': _L0_xcond_in['attn1_wv'], 'L0_xcond_attn1_wo': _L0_xcond_in['attn1_wo'], 'L0_xcond_attn1_bo': _L0_xcond_in['attn1_bo'], 'L0_xcond_attn2_wq': _L0_xcond_in['attn2_wq'], 'L0_xcond_attn2_wk': _L0_xcond_in['attn2_wk'], 'L0_xcond_attn2_wv': _L0_xcond_in['attn2_wv'], 'L0_xcond_attn2_wo': _L0_xcond_in['attn2_wo'], 'L0_xcond_attn2_bo': _L0_xcond_in['attn2_bo'], 'L0_xcond_ff_w1': _L0_xcond_in['ff_w1'], 'L0_xcond_ff_b1': _L0_xcond_in['ff_b1'], 'L0_xcond_ff_w2': _L0_xcond_in['ff_w2'], 'L0_xcond_ff_b2': _L0_xcond_in['ff_b2'], 'L0_xcond_norm1_w': _L0_xcond_in['norm1_w'], 'L0_xcond_norm1_b': _L0_xcond_in['norm1_b'], 'L0_xcond_norm2_w': _L0_xcond_in['norm2_w'], 'L0_xcond_norm2_b': _L0_xcond_in['norm2_b'], 'L0_xcond_norm3_w': _L0_xcond_in['norm3_w'], 'L0_xcond_norm3_b': _L0_xcond_in['norm3_b'], 'L0_ffn_router_w': _L0_ffn_in['router_w'], 'L0_ffn_w1': _L0_ffn_in['w1'], 'L0_ffn_w2': _L0_ffn_in['w2']}

def reference(x, cond_1024, ctx_1024, L0_xcond_attn1_wq, L0_xcond_attn1_wk, L0_xcond_attn1_wv, L0_xcond_attn1_wo, L0_xcond_attn1_bo, L0_xcond_attn2_wq, L0_xcond_attn2_wk, L0_xcond_attn2_wv, L0_xcond_attn2_wo, L0_xcond_attn2_bo, L0_xcond_ff_w1, L0_xcond_ff_b1, L0_xcond_ff_w2, L0_xcond_ff_b2, L0_xcond_norm1_w, L0_xcond_norm1_b, L0_xcond_norm2_w, L0_xcond_norm2_b, L0_xcond_norm3_w, L0_xcond_norm3_b, L0_ffn_router_w, L0_ffn_w1, L0_ffn_w2):
    import jax
    import jax.numpy as jnp

    def _L0_xcond_ref(x, t, context, attn1_wq, attn1_wk, attn1_wv, attn1_wo, attn1_bo, attn2_wq, attn2_wk, attn2_wv, attn2_wo, attn2_bo, ff_w1, ff_b1, ff_w2, ff_b2, norm1_w, norm1_b, norm2_w, norm2_b, norm3_w, norm3_b):
        import jax, jax.numpy as jnp
        import numpy as np
        import math
        B, S, CTX, D, H, DH = (2, 256, 32, 128, 16, 64)
        INNER = H * DH
        DFF = 4 * D

        def layernorm(x, eps=1e-05):
            m = jnp.mean(x, axis=-1, keepdims=True)
            v = jnp.var(x, axis=-1, keepdims=True)
            return (x - m) * jax.lax.rsqrt(v + eps)

        def adaln(x, t, w, b):
            emb = t @ w + b
            scale, shift = jnp.split(emb, 2, axis=-1)
            return layernorm(x) * (1.0 + scale) + shift

        def mha(xq, ctx, wq, wk, wv, wo, bo):
            b, sq, _ = xq.shape
            sk = ctx.shape[1]
            q = (xq @ wq).reshape(b, sq, H, DH).transpose(0, 2, 1, 3)
            k = (ctx @ wk).reshape(b, sk, H, DH).transpose(0, 2, 1, 3)
            v = (ctx @ wv).reshape(b, sk, H, DH).transpose(0, 2, 1, 3)
            scores = jnp.einsum('bhqd,bhkd->bhqk', q, k) / math.sqrt(DH)
            attn = jax.nn.softmax(scores, axis=-1)
            out = jnp.einsum('bhqk,bhkd->bhqd', attn, v)
            out = out.transpose(0, 2, 1, 3).reshape(b, sq, INNER)
            return out @ wo + bo

        def glu_ff(x, w1, b1, w2, b2):
            u = x @ w1 + b1
            a, gate = jnp.split(u, 2, axis=-1)
            return a * jax.nn.gelu(gate, approximate=False) @ w2 + b2
        h1 = adaln(x, t, norm1_w, norm1_b)
        x = mha(h1, h1, attn1_wq, attn1_wk, attn1_wv, attn1_wo, attn1_bo) + x
        h2 = adaln(x, t, norm2_w, norm2_b)
        x = mha(h2, context, attn2_wq, attn2_wk, attn2_wv, attn2_wo, attn2_bo) + x
        h3 = adaln(x, t, norm3_w, norm3_b)
        x = glu_ff(h3, ff_w1, ff_b1, ff_w2, ff_b2) + x
        return x

    def _L0_ffn_ref(x, router_w, w1, w2):
        import jax, jax.numpy as jnp
        import numpy as np
        HIDDEN = 128
        NUM_EXPERTS = 8
        TOP_K = 2
        bsz, seq, hidden = x.shape
        tokens = x.reshape(-1, hidden)
        logits = tokens @ router_w.T
        topk_vals, topk_idx = jax.lax.top_k(logits, TOP_K)
        weights = jax.nn.softmax(topk_vals, axis=-1)
        h = jnp.einsum('td,edf->etf', tokens, w1)
        h = jax.nn.gelu(h, approximate=False)
        out_all = jnp.einsum('etf,efd->etd', h, w2)
        out_ted = jnp.transpose(out_all, (1, 0, 2))
        gathered = jnp.take_along_axis(out_ted, topk_idx[:, :, None], axis=1)
        output = jnp.sum(weights[:, :, None] * gathered, axis=1)
        return output.reshape(bsz, seq, hidden)
    x = x + _L0_xcond_ref(_layernorm(x, axis=-1), cond_1024[:, None, :], ctx_1024, L0_xcond_attn1_wq, L0_xcond_attn1_wk, L0_xcond_attn1_wv, L0_xcond_attn1_wo, L0_xcond_attn1_bo, L0_xcond_attn2_wq, L0_xcond_attn2_wk, L0_xcond_attn2_wv, L0_xcond_attn2_wo, L0_xcond_attn2_bo, L0_xcond_ff_w1, L0_xcond_ff_b1, L0_xcond_ff_w2, L0_xcond_ff_b2, L0_xcond_norm1_w, L0_xcond_norm1_b, L0_xcond_norm2_w, L0_xcond_norm2_b, L0_xcond_norm3_w, L0_xcond_norm3_b)
    x = x + _L0_ffn_ref(_layernorm(x, axis=-1), L0_ffn_router_w, L0_ffn_w1, L0_ffn_w2)
    return x

_drawn_inputs = setup_inputs


def setup_inputs(seed=0):
    import zlib

    import numpy as np

    out = dict(_drawn_inputs(seed))
    spreads = {}
    factors = {'L0_xcond_attn1_bo': 8.0,
     'L0_xcond_attn2_bo': 23.744,
     'L0_xcond_ff_b1': 8.0,
     'L0_xcond_ff_b2': 25.795,
     'L0_xcond_norm1_b': 4.252,
     'L0_xcond_norm2_b': 8.0,
     'L0_xcond_norm3_b': 8.0}
    for name, (base, spread) in spreads.items():
        noise = np.random.default_rng([zlib.crc32(name.encode()), seed]).standard_normal(out[name].shape)
        drawn = base * np.exp(spread * noise) if base else spread * noise
        out[name] = jnp.asarray(drawn.astype(out[name].dtype))
    for name, factor in factors.items():
        out[name] = (out[name] * factor).astype(out[name].dtype)
    return out
```

```python
from contextlib import ExitStack

import concourse.bass as bass
from concourse import mybir

F32 = mybir.dt.float32
F32R = mybir.dt.float32r
U32 = mybir.dt.uint32
ALU = mybir.AluOpType
ACT = mybir.ActivationFunctionType
AX_X = mybir.AxisListType.X

P = 128
BANK = 512
RING = 4
EPS = 1e-5


def landed(k, u):
    return (k - u) * 8 + 16


def attention_phase(nc, name, sizes, mem, norm, weights, residual_bias, context):
    S, D, H, NG = sizes["S"], sizes["D"], sizes["H"], sizes["NG"]
    GT, NB, NP = 4 * S, 4, 2
    HC = BANK // S
    QC = BANK // D
    A_hi, A_lo, B = weights
    y, scale, shift, ident = mem["y"], mem["scale"], mem["shift"], mem["ident"]
    G_JOBS, T_JOBS, V_JOBS = H * GT // BANK, H // 2 // QC, 2 * (H // 2) // QC
    JOBS = G_JOBS + 2 * T_JOBS + 2 * V_JOBS

    with ExitStack() as ctx:
        def sb(n, shape, dt=F32):
            return ctx.enter_context(nc.sbuf_tensor(f"{name}_{n}", shape, dt))

        def ps(n, shape):
            return ctx.enter_context(nc.psum_tensor(f"{name}_{n}", shape, F32))

        def sem(n):
            return ctx.enter_context(nc.semaphore(f"{name}_{n}"))

        z = [sb(f"z{u}", [P, 2, D]) for u in range(2)]
        hT = [sb(f"hT{u}", [D, GT]) for u in range(2)]
        sT = [sb(f"sT{u}", [D, GT]) for u in range(2)] if context is not None else hT
        s_hi_buf = [sb(f"s_hi{u}", [D, GT], F32R) for u in range(2)]
        s_lo_buf = [sb(f"s_lo{u}", [D, GT], F32R) for u in range(2)]
        c_in = [sb(f"c_in{u}", [P, 2, D]) for u in range(2)] if context is not None else None
        G = sb("G", [D, H, GT])
        V = [sb(f"V{u}", [P, NB, H // 2, D]) for u in range(2)]
        Pr = [[sb(f"P{u}{p}", [P, H, S]) for p in range(NP)] for u in range(2)]
        PT = sb("PT", [P, NP, H // 2, P])
        stats = sb("stats", [P, 2, 6])
        mv = sb("mv", [P, 2, 2])
        var = sb("var", [P, 2])
        rstd = sb("rstd", [P, 2])
        top = sb("top", [P, H])
        total = sb("total", [P, H])
        inv = [sb(f"inv{p}", [P, H]) for p in range(NP)]

        ring = [ps(f"ring{i}", [P, BANK]) for i in range(RING)]
        Sps = ps("S", [P, 2 * BANK])
        tps = ps("tps", [P, BANK])
        ops = ps("ops", [P, BANK])

        s_ctx = [sem(f"ctx_loaded{u}") for u in range(2)]
        s_stats0 = sem("stats0")
        s_stats = sem("stats")
        s_aggr = sem("aggr")
        s_var = sem("var")
        s_rstd = sem("rstd")
        s_yb = sem("y_bias")
        s_z = sem("z")
        s_tps = sem("tps")
        s_hf = sem("hf")
        s_hi = sem("hi")
        s_h = sem("h")
        s_full = sem("ring_full")
        s_free = sem("ring_free")
        s_S = sem("scores")
        s_top = sem("top")
        s_sub = sem("sub")
        s_exp = sem("exp")
        s_sum = sem("sum")
        s_inv = sem("inv")
        s_P = sem("P")
        s_o = sem("o")
        s_y = sem("y")

        block = ctx.enter_context(nc.Block())

        def turn(step, local):
            return local if isinstance(step, int) and step == 0 else step * JOBS + (local - 2 * T_JOBS)

        def locals_of(step):
            if isinstance(step, int) and step == 0:
                return [G_JOBS, G_JOBS + V_JOBS], None
            if isinstance(step, int) and step == NG:
                return None, [0, T_JOBS]
            t0 = G_JOBS
            return [t0 + T_JOBS, t0 + 2 * T_JOBS + V_JOBS], [t0, t0 + T_JOBS + V_JOBS]

        def steps(eng, body):
            body(0, 0)
            with eng.Fori(0, NG - 5, 2) as i:
                body(i + 1, 1)
                body(i + 2, 0)
            for g in range(NG - 3, NG + 1):
                body(g, g % 2)

        if context is not None:
            @block.sync
            def _(sp):
                def load(k, u):
                    sp.dma_start(c_in[u][:], context[bass.ds(k * 2, 2)].rearrange("t p d -> p t d")).then_inc(s_ctx[u], 16)
                load(0, 0)
                load(1, 1)

                def later(k, u):
                    sp.wait_ge(s_tps, k - 1)
                    load(k, u)
                with sp.Fori(0, NG - 3, 2) as i:
                    later(i + 2, 0)
                    later(i + 3, 1)

        @block.gpsimd
        def _(pool):
            def rstd_of(k):
                pool.wait_ge(s_var, k + 1)
                nc.gpsimd.tensor_tensor(rstd[:], var[:], mem["neg_half"][:, 0:2], ALU.pow).then_inc(s_rstd, 1)

            def normalise(g, u, p):
                pool.wait_ge(s_inv, g * 2 + (p + 1))
                pr = Pr[u][p]
                nc.gpsimd.tensor_tensor(pr[:], pr[:], inv[p][:].unsqueeze(2).to_broadcast([P, H, S]),
                                        ALU.mult).then_inc(s_P, 1)

            rstd_of(0)
            rstd_of(1)

            def body(g, u):
                last = isinstance(g, int)
                if not (last and g >= NG - 2):
                    rstd_of(g + 2)
                if not (last and g == NG):
                    for p in range(NP):
                        normalise(g, u, p)
            steps(pool, body)

        @block.scalar
        def _(act):
            def copy_out(step, local, out):
                n = turn(step, local)
                act.wait_ge(s_full, n + 1)
                src = ring[local % RING][:]
                nc.scalar.copy(out, src).then_inc(s_free, 1)

            def exps(g, u, p):
                act.wait_ge(s_sub, g * 2 + (p + 1))
                nc.scalar.activation(Pr[u][p][:], Pr[u][p][:], ACT.Exp).then_inc(s_exp, 1)

            def body(g, u):
                last = isinstance(g, int) and g == NG
                values, transposed = locals_of(g)
                if not last:
                    for j in range(G_JOBS):
                        copy_out(g, j, G[:, 2 * j:2 * j + 2, :])
                for p in range(NP):
                    if transposed:
                        for c in range(T_JOBS):
                            copy_out(g, transposed[p] + c, PT[:, p, QC * c:QC * c + QC, :])
                    if not last:
                        for i in range(V_JOBS):
                            if i == V_JOBS - 1:
                                exps(g, u, p)
                            copy_out(g, values[p] + i, V[u][:, 2 * p + i // T_JOBS, QC * (i % T_JOBS):QC * (i % T_JOBS) + QC, :])
            steps(act, body)

        @block.vector
        def _(dve):
            def statistics(k):
                for t in range(2):
                    ins = nc.vector.bn_stats(stats[:, t, :], y[:, bass.ds(k * 2 + t, 1), :])
                if isinstance(k, int) and k == 0:
                    ins.then_inc(s_stats0, 1)
                    dve.wait_ge(s_stats0, 1)
                else:
                    ins.then_inc(s_stats, 1)
                    dve.wait_ge(s_stats, 1)
                    dve.wait_ge(s_stats, k)
                for t in range(2):
                    ins = nc.vector.bn_aggr(mv[:, t, :], stats[:, t, :])
                ins.then_inc(s_aggr, 1)
                dve.wait_ge(s_aggr, k + 1)
                nc.vector.tensor_scalar(var[:], mv[:, :, 1], EPS, None, ALU.add).then_inc(s_var, 1)

            def normalised(k, u):
                dve.wait_ge(s_rstd, k + 1)
                for t in range(2):
                    ins = nc.vector.tensor_scalar(z[u][:, t:t + 1, :], y[:, bass.ds(k * 2 + t, 1), :], mv[:, t, 0:1],
                                                  rstd[:, t:t + 1], ALU.subtract, ALU.mult)
                ins.then_inc(s_z, 1)
                dve.wait_ge(s_z, k + 1)
                yk = y[:, bass.ds(k * 2, 2), :]
                nc.vector.tensor_tensor(yk, yk, residual_bias.unsqueeze(1).to_broadcast([P, 2, D]),
                                        ALU.add).then_inc(s_yb, 1)

            def modulate(k, u):
                dve.wait_ge(s_tps, k + 1)
                if context is not None:
                    nc.vector.tensor_copy(sT[u][:], tps[:, GT:2 * GT])
                for b in range(NB):
                    ins = nc.vector.tensor_scalar(hT[u][:, S * b:S * b + S], tps[:, S * b:S * b + S],
                                                  scale[:, norm, bass.ds(k * NB + b, 1)],
                                                  shift[:, norm, bass.ds(k * NB + b, 1)], ALU.mult, ALU.add)
                ins.then_inc(s_hf, 1)
                dve.wait_ge(s_hf, k + 1)
                nc.vector.tensor_copy(s_hi_buf[u][:], sT[u][:]).then_inc(s_hi, 1)
                dve.wait_ge(s_hi, k + 1)
                nc.vector.tensor_tensor(s_lo_buf[u][:], sT[u][:], s_hi_buf[u][:].bitcast(F32), ALU.subtract).then_inc(s_h, 1)

            def subtract_max(g, u, p):
                dve.wait_ge(s_S, g * 2 + (p + 1))
                sc = Sps[:].rearrange("q (h k) -> q h k", k=S)
                nc.vector.tensor_reduce(top[:], sc, AX_X, ALU.max).then_inc(s_top, 1)
                dve.wait_ge(s_top, g * 2 + (p + 1))
                nc.vector.tensor_tensor(Pr[u][p][:], sc, top[:].unsqueeze(2).to_broadcast([P, H, S]),
                                        ALU.subtract).then_inc(s_sub, 1)

            def sums(g, u, p):
                dve.wait_ge(s_exp, g * 2 + (p + 1))
                nc.vector.tensor_reduce(total[:], Pr[u][p][:], AX_X, ALU.add).then_inc(s_sum, 1)
                dve.wait_ge(s_sum, g * 2 + (p + 1))
                nc.vector.reciprocal(inv[p][:], total[:]).then_inc(s_inv, 1)

            def residual(g, p):
                dve.wait_ge(s_o, g * 2 + (p + 1))
                if p == 0:
                    dve.wait_ge(s_yb, g + 1)
                yt = y[:, bass.ds(g * 2 + p, 1), :]
                nc.vector.tensor_tensor(yt, ops[:, 0:D].unsqueeze(1), yt, ALU.add).then_inc(s_y, 1)

            statistics(0)
            normalised(0, 0)
            statistics(1)
            modulate(0, 0)
            normalised(1, 1)

            def body(g, u):
                static = isinstance(g, int)
                ahead2 = not (static and g >= NG - 2)
                ahead1 = not (static and g >= NG - 1)
                now = not (static and g >= NG)
                behind = not (static and g == 0)
                if ahead2:
                    statistics(g + 2)
                if now:
                    subtract_max(g, u, 0)
                if behind:
                    residual(g - 1, 0)
                if now:
                    sums(g, u, 0)
                    subtract_max(g, u, 1)
                if ahead2:
                    normalised(g + 2, u)
                if ahead1:
                    modulate(g + 1, 1 - u)
                if now:
                    sums(g, u, 1)
                if behind:
                    residual(g - 1, 1)
            steps(dve, body)

        @block.tensor
        def _(pe):
            def turned(step, local):
                n = turn(step, local)
                if not (isinstance(n, int) and n < RING):
                    pe.wait_ge(s_free, n - (RING - 1))
                return ring[local % RING]

            def transpose_tokens(k, u):
                pe.wait_ge(s_z, k + 1)
                if context is not None:
                    pe.wait_ge(s_ctx[u], landed(k, u))
                if not (isinstance(k, int) and k == 0):
                    pe.wait_ge(s_hf, k)
                for t in range(2):
                    ins = nc.tensor.transpose(tps[:, P * t:P * t + P], z[u][:, t, :], ident[:])
                if context is not None:
                    for t in range(2):
                        ins = nc.tensor.transpose(tps[:, GT + P * t:GT + P * t + P], c_in[u][:, t, :], ident[:])
                ins.then_inc(s_tps, 1)

            def keys(g, u):
                pe.wait_ge(s_h, g + 1)
                for j in range(G_JOBS):
                    bank = turned(g, j)
                    for i in range(2):
                        out, h = bank[:, GT * i:GT * i + GT], 2 * j + i
                        nc.tensor.matmul(out, A_hi[:, h, :], s_hi_buf[u][:], start=True, stop=False)
                        nc.tensor.matmul(out, A_hi[:, h, :], s_lo_buf[u][:], start=False, stop=False)
                        ins = nc.tensor.matmul(out, A_lo[:, h, :], s_hi_buf[u][:], start=False, stop=True)
                    ins.then_inc(s_full, 1)

            def scores(g, u, p):
                pe.wait_ge(s_free, turn(g, G_JOBS))
                if not (isinstance(g, int) and g == 0 and p == 0):
                    pe.wait_ge(s_sub, g * 2 + p)
                for c in range(H // HC):
                    for b in range(2):
                        tok = slice(S * (2 * p + b), S * (2 * p + b) + S)
                        ins = nc.tensor.matmul(Sps[S * b:S * b + S, BANK * c:BANK * c + BANK], hT[u][:, tok],
                                               G[:, HC * c:HC * c + HC, tok], start=True, stop=True)
                ins.then_inc(s_S, 1)

            def values(g, u, p, local):
                for i in range(V_JOBS):
                    b, c = 2 * p + i // T_JOBS, i % T_JOBS
                    bank = turned(g, local + i)
                    for par in range(2):
                        ins = nc.tensor.matmul(bank[S * par:S * par + S, :], sT[u][:, S * b:S * b + S],
                                               B[:, par, QC * c:QC * c + QC, :], start=True, stop=True)
                    ins.then_inc(s_full, 1)

            def transpose_probabilities(g, u, p, step, local):
                pe.wait_ge(s_P, g * 2 + (p + 1))
                pr = Pr[u][p][:].rearrange("q h k -> q (h k)")
                for c in range(T_JOBS):
                    bank = turned(step, local + c)
                    for i in range(QC):
                        n = QC * c + i
                        ins = nc.tensor.transpose(bank[:, P * i:P * i + P], pr[:, P * n:P * n + P], ident[:])
                    ins.then_inc(s_full, 1)

            def weighted_sum(g, u, p, step, local):
                pe.wait_ge(s_free, turn(step, local + T_JOBS))
                if not (isinstance(g, int) and g == 0 and p == 0):
                    pe.wait_ge(s_y, g * 2 + p)
                for n in range(H // 2):
                    for b in range(2):
                        ins = nc.tensor.matmul(ops[S * b:S * b + S, 0:D], PT[:, p, n, S * b:S * b + S],
                                               V[u][:, 2 * p + b, n, :], start=n == 0, stop=n == H // 2 - 1)
                ins.then_inc(s_o, 1)

            transpose_tokens(0, 0)

            def body(g, u):
                static = isinstance(g, int)
                now = not (static and g >= NG)
                ahead = not (static and g >= NG - 1)
                vl, tl = locals_of(g)
                if now:
                    keys(g, u)
                if tl:
                    transpose_probabilities(g - 1, 1 - u, 0, g, tl[0])
                if now:
                    scores(g, u, 0)
                    values(g, u, 0, vl[0])
                if tl:
                    weighted_sum(g - 1, 1 - u, 0, g, tl[0])
                    transpose_probabilities(g - 1, 1 - u, 1, g, tl[1])
                if now:
                    scores(g, u, 1)
                if ahead:
                    transpose_tokens(g + 1, 1 - u)
                if now:
                    values(g, u, 1, vl[1])
                if tl:
                    weighted_sum(g - 1, 1 - u, 1, g, tl[1])
            steps(pe, body)


def setup_phase(nc, sizes, mem, inputs):
    S, D, H, NG, BATCH = sizes["S"], sizes["D"], sizes["H"], sizes["NG"], sizes["BATCH"]
    HP = H // 2
    NT = 2 * NG
    XC = 4
    dh = S
    y, scale, shift, ident = mem["y"], mem["scale"], mem["shift"], mem["ident"]

    with ExitStack() as ctx:
        def sb(n, shape, dt=F32):
            return ctx.enter_context(nc.sbuf_tensor(f"set_{n}", shape, dt))

        def sem(n):
            return ctx.enter_context(nc.semaphore(f"set_{n}"))

        x = sb("x", [P, NT, D])
        NR6 = BATCH + 6
        rows = sb("rows", [NR6, D])
        rowsT = sb("rowsT", [D, NR6])
        nw = sb("nw", [D, 3, 2 * D])
        biases = sb("biases", [1, 3, D])
        ones = sb("ones", [1, P])
        w_in = [[sb(f"w{m}{a}", [D, H * dh]) for m in range(3)] for a in range(2)]
        wo = [sb(f"wo{a}", [P, HP, D]) for a in range(2)]
        wT = [sb(f"wT{m}", [P, HP, D]) for m in range(3)]
        stats = sb("stats", [P, NT, 6])
        mv = sb("mv", [P, NT, 2])
        var = sb("var", [P, NT])
        rstd = sb("rstd", [P, NT])
        ring = [ctx.enter_context(nc.psum_tensor(f"set_ring{i}", [P, BANK], F32)) for i in range(8)]
        misc, ring = ring[6:], ring[:6]
        NR = len(ring)

        s_x = [sem(f"x{i}") for i in range(XC)]
        s_cond = sem("cond_loaded")
        s_w = [sem(f"w_loaded{a}") for a in range(2)]
        s_ident = sem("ident")
        s_ones = sem("ones")
        s_half = sem("half")
        s_condT = sem("condT")
        s_cT = sem("cT")
        s_emb = sem("emb")
        s_bias = sem("bias")
        s_stats = sem("stats")
        s_aggr = sem("aggr")
        s_var = sem("var")
        s_rstd = sem("rstd")
        s_full = sem("full")
        s_free = sem("free")
        s_lo = sem("lo")
        block = ctx.enter_context(nc.Block())

        TB = HP * P // BANK
        AB = H * D // BANK
        PB = BANK // P
        A_TURNS = 3 * TB + 2 * AB

        @block.sync
        def _(sp):
            sp.dma_start(rows[0:BATCH, :], inputs["cond"]).then_inc(s_cond, 16)
            for i in range(3):
                sp.dma_start(nw[:, i, :], inputs[f"norm{i + 1}_w"]).then_inc(s_cond, 16)
                sp.dma_start(rows[BATCH + 2 * i:BATCH + 2 * i + 2, :],
                             inputs[f"norm{i + 1}_b"].rearrange("(c p) -> c p", p=D)).then_inc(s_cond, 16)
            for i, n in enumerate(("attn1_bo", "attn2_bo", "ff_b2")):
                sp.dma_start(biases[:, i, :], inputs[n].rearrange("(a n) -> a n", a=1)).then_inc(s_cond, 16)
            for a in range(2):
                for m, n in enumerate(("wq", "wk", "wv")):
                    sp.dma_start(w_in[a][m][:], inputs[f"attn{a + 1}_{n}"]).then_inc(s_w[a], 16)
                sp.dma_start(wo[a][:], inputs[f"attn{a + 1}_wo"].rearrange("(h p) d -> p h d", p=P)).then_inc(s_w[a], 16)

        @block.gpsimd
        def _(pool):
            nc.gpsimd.memset(ident[:], 0.0).then_inc(s_ident, 1)
            pool.wait_ge(s_ident, 1)
            nc.gpsimd.affine_select(out=ident[:], in_=ident[:], compare_op=ALU.not_equal, fill=1.0, base=0,
                                    pattern=[[-1, P]], channel_multiplier=1).then_inc(s_ident, 1)
            nc.gpsimd.memset(ones[:], 1.0).then_inc(s_ones, 1)
            nc.gpsimd.memset(mem["neg_half"][:], -0.5).then_inc(s_half, 1)
            pool.wait_ge(s_half, 1)
            pool.wait_ge(s_var, 1)
            nc.gpsimd.tensor_tensor(rstd[:], var[:], mem["neg_half"][:], ALU.pow).then_inc(s_rstd, 1)

        @block.scalar
        def _(act):
            per = NT // XC
            for i in range(XC):
                act.dma_start(x[:, i * per:i * per + per, :],
                              inputs["x"][i * per:i * per + per].rearrange("t p d -> p t d")).then_inc(s_x[i], 16)
            for a in range(2):
                A_hi, _, B = mem["attn"][a]
                n = a * A_TURNS
                for m in range(3):
                    for c in range(TB):
                        act.wait_ge(s_full, n + 1)
                        nc.scalar.copy(wT[m][:, PB * c:PB * c + PB, :], ring[n % NR][:]).then_inc(s_free, 1)
                        n += 1
                for par in range(2):
                    for c in range(AB // 2):
                        act.wait_ge(s_full, n + 1)
                        out = A_hi[:].rearrange("p (n two) d -> p n two d", two=2)[:, PB * c:PB * c + PB, par, :]
                        nc.scalar.activation(out, ring[n % NR][:].rearrange("p (n d) -> p n d", d=D), ACT.Copy,
                                             scale=dh ** -0.5).then_inc(s_free, 1)
                        n += 1
                for par in range(2):
                    for c in range(AB // 2):
                        act.wait_ge(s_full, n + 1)
                        nc.scalar.copy(B[:, par, PB * c:PB * c + PB, :], ring[n % NR][:]).then_inc(s_free, 1)
                        n += 1

        @block.vector
        def _(dve):
            dve.wait_ge(s_condT, 1)
            nc.vector.tensor_copy(rowsT[:], misc[0][:, 0:NR6]).then_inc(s_cT, 1)
            dve.wait_ge(s_emb, 1)
            for i in range(3):
                nb = rowsT[:, BATCH + 2 * i:BATCH + 2 * i + 2]
                src = misc[1][:, 2 * BATCH * i:2 * BATCH * i + 2 * BATCH]
                nc.vector.tensor_scalar(scale[:, i, :], src[:, 0:BATCH], nb[:, 0:1], 1.0, ALU.add, ALU.add)
                nc.vector.tensor_scalar(shift[:, i, :], src[:, BATCH:], nb[:, 1:2], None, ALU.add)
            dve.wait_ge(s_bias, 1)
            nc.vector.tensor_copy(mem["bias"][:], misc[0][:, 0:3 * D])

            def low_parts(a):
                A_hi, A_lo, _ = mem["attn"][a]
                for i in range(AB):
                    par, c = i // (AB // 2), i % (AB // 2)
                    n = a * A_TURNS + 3 * TB + i
                    dve.wait_ge(s_free, n + 1)
                    pick = lambda A: A[:].rearrange("p (n two) d -> p n two d", two=2)[:, PB * c:PB * c + PB, par, :]
                    nc.vector.scalar_tensor_tensor(out=pick(A_lo), in0=ring[n % NR][:].rearrange("p (n d) -> p n d", d=D),
                                                   scalar=dh ** -0.5, in1=pick(A_hi).bitcast(F32),
                                                   op0=ALU.mult, op1=ALU.subtract).then_inc(s_lo, 1)
            low_parts(0)
            for i in range(XC):
                dve.wait_ge(s_x[i], 16)
                for t in range(i * NT // XC, (i + 1) * NT // XC):
                    nc.vector.bn_stats(stats[:, t, :], x[:, t, :]).then_inc(s_stats, 1)
            dve.wait_ge(s_stats, NT)
            for t in range(NT):
                nc.vector.bn_aggr(mv[:, t, :], stats[:, t, :]).then_inc(s_aggr, 1)
            dve.wait_ge(s_aggr, NT)
            nc.vector.tensor_scalar(var[:], mv[:, :, 1], EPS, None, ALU.add).then_inc(s_var, 1)
            low_parts(1)
            dve.wait_ge(s_rstd, 1)
            for t in range(NT):
                nc.vector.tensor_scalar(y[:, t, :], x[:, t, :], mv[:, t, 0:1], rstd[:, t:t + 1], ALU.subtract, ALU.mult)

        @block.tensor
        def _(pe):
            pe.wait_ge(s_ident, 2)
            pe.wait_ge(s_ones, 1)
            pe.wait_ge(s_cond, 16 * 10)
            nc.tensor.transpose(misc[0][:, 0:NR6], rows[:], ident[0:NR6, 0:NR6]).then_inc(s_condT, 1)
            pe.wait_ge(s_cT, 1)
            for i in range(3):
                for c in range(2):
                    o = BATCH * (2 * i + c)
                    ins = nc.tensor.matmul(misc[1][:, o:o + BATCH], nw[:, i, D * c:D * c + D], rowsT[:, 0:BATCH], start=True, stop=True)
            ins.then_inc(s_emb, 1)
            nc.tensor.matmul(misc[0][:, 0:3 * D], ones[:], biases[:].rearrange("a b d -> a (b d)"),
                             start=True, stop=True).then_inc(s_bias, 1)

            def turned(n, of_a):
                if n >= NR:
                    pe.wait_ge(s_free, n - NR + 1)
                if of_a:
                    pe.wait_ge(s_lo, of_a)
                return ring[n % NR]

            def a_before(n):
                m = n - NR + 1
                return sum(min(max(m - a * A_TURNS - 3 * TB, 0), AB) for a in range(2))

            for a in range(2):
                n = a * A_TURNS
                pe.wait_ge(s_w[a], 64)
                for m in range(3):
                    for c in range(TB):
                        bank = turned(n, a_before(n))
                        for i in range(PB):
                            k = PB * c + i
                            ins = nc.tensor.transpose(bank[:, P * i:P * i + P], w_in[a][m][:, P * k:P * k + P], ident[:])
                        ins.then_inc(s_full, 1)
                        n += 1
                pe.wait_ge(s_free, n)
                for left, right in ((wT[1], wT[0]), (wT[2], wo[a])):
                    for par in range(2):
                        half = slice(dh * par, dh * par + dh)
                        for c in range(AB // 2):
                            bank = turned(n, a_before(n))
                            for i in range(PB):
                                k = PB * c + i
                                ins = nc.tensor.matmul(bank[:, D * i:D * i + D], left[half, k, :], right[half, k, :],
                                                       start=True, stop=True)
                            ins.then_inc(s_full, 1)
                            n += 1


def feed_forward_phase(nc, sizes, mem, inputs, out):
    S, D, NG = sizes["S"], sizes["D"], sizes["NG"]
    E, F = sizes["E"], sizes["F"]
    DFF = sizes["DFF"]
    GT, NB = 4 * S, 4
    FB, EB = DFF // P, F // P
    y, scale, shift, ident = mem["y"], mem["scale"], mem["shift"], mem["ident"]
    norm = 2

    with ExitStack() as ctx:
        def sb(n, shape, dt=F32):
            return ctx.enter_context(nc.sbuf_tensor(f"ff_{n}", shape, dt))

        def ps(n, shape):
            return ctx.enter_context(nc.psum_tensor(f"ff_{n}", shape, F32))

        def sem(n):
            return ctx.enter_context(nc.semaphore(f"ff_{n}"))

        w1 = sb("w1", [D, 2 * DFF])
        w1_hi = sb("w1_hi", [D, 2 * DFF], F32R)
        w1_lo = sb("w1_lo", [D, 2 * DFF], F32R)
        w2 = sb("w2", [P, FB, D])
        e1 = sb("e1", [D, E, F])
        e1_hi = sb("e1_hi", [D, E, F], F32R)
        e1_lo = sb("e1_lo", [D, E, F], F32R)
        e2 = sb("e2", [P, E, EB, D])
        rows = sb("rows", [E + 2 * FB, D])
        rowsT = sb("rowsT", [D, E + 2 * FB])
        routerT, b1 = rowsT[:, 0:E], rowsT[:, E:]
        iota = sb("iota", [P, E])
        euler = sb("euler", [P, 2])
        z = [sb(f"z{u}", [P, 2, D]) for u in range(2)]
        hT = sb("hT", [D, GT])
        h_hi = sb("h_hi", [D, GT], F32R)
        h_lo = sb("h_lo", [D, GT], F32R)
        gate = sb("gate", [P, 2, GT])
        hid = sb("hid", [P, FB, GT])
        x = [sb(f"x{u}", [P, 2, D]) for u in range(2)]
        xn = sb("xn", [P, 2, D])
        xT = [sb(f"xT{u}", [D, GT]) for u in range(2)]
        x_hi = [sb(f"x_hi{u}", [D, GT], F32R) for u in range(2)]
        x_lo = [sb(f"x_lo{u}", [D, GT], F32R) for u in range(2)]
        eh = [sb(f"eh{i}", [P, EB, GT]) for i in range(E)]
        stats = sb("stats", [P, 2, 6])
        mv = sb("mv", [P, 2, 2])
        var = sb("var", [P, 2])
        rstd = sb("rstd", [P, 2])
        xstats = sb("xstats", [P, 2, 6])
        xmv = sb("xmv", [P, 2, 2])
        xvar = sb("xvar", [P, 2])
        xrstd = sb("xrstd", [P, 2])
        logits = sb("logits", [P, 2, E])
        best = sb("best", [P, 2, 8])
        place = sb("place", [P, 2, 8], U32)
        placef = sb("placef", [P, 2, 2])
        diff = sb("diff", [P, 2])
        ratio = sb("ratio", [P, 2])
        denom = sb("denom", [P, 2])
        p1 = sb("p1", [P, 2])
        p2 = sb("p2", [P, 2])
        second = sb("second", [P, 2, E])
        mix = [sb(f"mix{u}", [P, 2, E]) for u in range(2)]

        tps = ps("tps", [P, BANK])
        xps = ps("xps", [P, BANK])
        fps = [ps(f"fps{i}", [P, BANK]) for i in range(2)]
        hps = [ps(f"hps{i}", [P, BANK]) for i in range(2)]
        ops = [ps(f"ops{i}", [P, BANK]) for i in range(2)]
        OB = BANK // D
        O_JOBS = 2 * E // OB

        s_w = sem("weights")
        s_x = [sem(f"x_loaded{u}") for u in range(2)]
        s_const = sem("const")
        s_rt = sem("router_t")
        s_whi = sem("w_hi")
        s_wr = sem("w_ready")
        s_stats0 = sem("stats0")
        s_stats = sem("stats")
        s_aggr = sem("aggr")
        s_var = sem("var")
        s_rstd = sem("rstd")
        s_z = sem("z")
        s_yb = sem("yb")
        s_tps = sem("tps")
        s_hf = sem("hf")
        s_hi = sem("hi")
        s_h = sem("h")
        s_u = sem("u")
        s_gate = sem("gate")
        s_hid = sem("hid")
        s_ff = sem("ff")
        s_y = sem("y")
        s_xy = sem("xy")
        s_xs = sem("xs")
        s_xa = sem("xa")
        s_xv = sem("xv")
        s_xr = sem("xr")
        s_xn = sem("xn")
        s_xps = sem("xps")
        s_xf = sem("xf")
        s_xhi = sem("xhi")
        s_xT = sem("xT")
        s_lg = sem("lg")
        s_lgs = sem("lgs")
        s_best = sem("best")
        s_place = sem("place")
        s_ratio = sem("ratio")
        s_soft = sem("soft")
        s_mix = sem("mix")
        s_eh = sem("eh_psum")
        s_eg = sem("eh")
        s_eo = sem("eo")
        s_acc = sem("acc")
        s_out = [sem(f"out{u}") for u in range(2)]
        block = ctx.enter_context(nc.Block())

        def steps(eng, body):
            body(-1, 1)
            body(0, 0)
            with eng.Fori(0, NG - 5, 2) as i:
                body(i + 1, 1)
                body(i + 2, 0)
            for g in range(NG - 3, NG):
                body(g, g % 2)

        @block.sync
        def _(sp):
            sp.dma_start(w1[:], inputs["ff_w1"]).then_inc(s_w, 16)
            sp.dma_start(e1[:], inputs["e_w1"].rearrange("e d f -> d e f")).then_inc(s_w, 16)
            sp.dma_start(rows[E:, :], inputs["ff_b1"].rearrange("(c p) -> c p", p=P)).then_inc(s_w, 16)
            sp.dma_start(w2[:], inputs["ff_w2"].rearrange("(c p) d -> p c d", p=P)).then_inc(s_w, 16)
            sp.dma_start(e2[:], inputs["e_w2"].rearrange("e (c p) d -> p e c d", p=P)).then_inc(s_w, 16)
            sp.dma_start(rows[0:E, :], inputs["router_w"]).then_inc(s_w, 16)

            def load(k, u):
                sp.dma_start(x[u][:], inputs["x"][bass.ds(k * 2, 2)].rearrange("t p d -> p t d")).then_inc(s_x[u], 16)

            def body(g, u):
                if isinstance(g, int) and g >= NG - 1:
                    return
                if not (isinstance(g, int) and g < 1):
                    sp.wait_ge(s_out[1 - u], landed(g - 1, 1 - u))
                load(g + 1, 1 - u)
            steps(sp, body)

        @block.gpsimd
        def _(pool):
            nc.gpsimd.iota(iota[:], [[1, E]], base=0, channel_multiplier=0,
                           allow_small_or_imprecise_dtypes=True).then_inc(s_const, 1)
            nc.gpsimd.memset(euler[:], 2.718281828459045).then_inc(s_const, 1)
            pool.wait_ge(s_const, 2)

            def rstd_of(k):
                pool.wait_ge(s_var, k + 1)
                nc.gpsimd.tensor_tensor(rstd[:], var[:], mem["neg_half"][:, 0:2], ALU.pow).then_inc(s_rstd, 1)

            rstd_of(0)
            rstd_of(1)

            def body(g, u):
                if not (isinstance(g, int) and (g < 0 or g >= NG - 2)):
                    rstd_of(g + 2)
                if not (isinstance(g, int) and g >= NG - 1):
                    pool.wait_ge(s_xv, g + 2)
                    nc.gpsimd.tensor_tensor(xrstd[:], xvar[:], mem["neg_half"][:, 0:2], ALU.pow).then_inc(s_xr, 1)
                    pool.wait_ge(s_place, g + 2)
                    nc.gpsimd.tensor_tensor(ratio[:], euler[:], diff[:], ALU.pow).then_inc(s_ratio, 1)
            steps(pool, body)

        @block.scalar
        def _(act):
            act.wait_ge(s_w, 16 * 6)
            nc.scalar.copy(w1_hi[:], w1[:]).then_inc(s_whi, 1)
            nc.scalar.copy(e1_hi[:], e1[:]).then_inc(s_whi, 1)

            act.wait_ge(s_wr, 3)

            def gates(k, c):
                act.wait_ge(s_u, k * FB + (c + 1))
                if not (isinstance(k, int) and k == 0 and c < 2):
                    act.wait_ge(s_hid, k * FB + (c - 1))
                nc.scalar.activation(gate[:, c % 2, :], fps[c % 2][:, 0:GT], ACT.Gelu,
                                     bias=b1[:, FB + c:FB + c + 1]).then_inc(s_gate, 1)

            def expert(g, e):
                act.wait_ge(s_eh, g * E + (e + 1))
                nc.scalar.activation(eh[e][:], hps[e % 2][:], ACT.Gelu).then_inc(s_eg, 1)

            def body(g, u):
                static = isinstance(g, int)
                if not (static and g >= NG - 1):
                    for c in range(FB):
                        gates(g + 1, c)
                if not (static and g < 0):
                    for e in range(E):
                        expert(g, e)
                    act.wait_ge(s_acc, g * 2 * E + 2 * E)
                    act.dma_start(out[bass.ds(g * 2, 2)].rearrange("t p d -> p t d"), x[u][:]).then_inc(s_out[u], 16)
            steps(act, body)
            for u in range(2):
                act.wait_ge(s_out[u], landed(NG - 2 + u, u))

        @block.vector
        def _(dve):
            dve.wait_ge(s_whi, 1)
            nc.vector.tensor_tensor(w1_lo[:], w1[:], w1_hi[:].bitcast(F32), ALU.subtract).then_inc(s_wr, 1)
            dve.wait_ge(s_whi, 2)
            nc.vector.tensor_tensor(e1_lo[:], e1[:], e1_hi[:].bitcast(F32), ALU.subtract).then_inc(s_wr, 1)
            dve.wait_ge(s_rt, 1)
            nc.vector.tensor_copy(rowsT[:], xps[:, 0:E + 2 * FB]).then_inc(s_wr, 1)
            dve.wait_ge(s_const, 2)

            def statistics(k):
                for t in range(2):
                    ins = nc.vector.bn_stats(stats[:, t, :], y[:, bass.ds(k * 2 + t, 1), :])
                if isinstance(k, int) and k == 0:
                    ins.then_inc(s_stats0, 1)
                    dve.wait_ge(s_stats0, 1)
                else:
                    ins.then_inc(s_stats, 1)
                    dve.wait_ge(s_stats, 1)
                    dve.wait_ge(s_stats, k)
                for t in range(2):
                    ins = nc.vector.bn_aggr(mv[:, t, :], stats[:, t, :])
                ins.then_inc(s_aggr, 1)
                dve.wait_ge(s_aggr, k + 1)
                nc.vector.tensor_scalar(var[:], mv[:, :, 1], EPS, None, ALU.add).then_inc(s_var, 1)

            def normalised(k, u):
                dve.wait_ge(s_rstd, k + 1)
                for t in range(2):
                    ins = nc.vector.tensor_scalar(z[u][:, t:t + 1, :], y[:, bass.ds(k * 2 + t, 1), :], mv[:, t, 0:1],
                                                  rstd[:, t:t + 1], ALU.subtract, ALU.mult)
                ins.then_inc(s_z, 1)
                dve.wait_ge(s_z, k + 1)
                yk = y[:, bass.ds(k * 2, 2), :]
                nc.vector.tensor_tensor(yk, yk, mem["bias"][:, norm * D:norm * D + D].unsqueeze(1).to_broadcast([P, 2, D]),
                                        ALU.add).then_inc(s_yb, 1)

            def modulate(k):
                dve.wait_ge(s_tps, k + 1)
                for b in range(NB):
                    ins = nc.vector.tensor_scalar(hT[:, S * b:S * b + S], tps[:, S * b:S * b + S],
                                                  scale[:, norm, bass.ds(k * NB + b, 1)],
                                                  shift[:, norm, bass.ds(k * NB + b, 1)], ALU.mult, ALU.add)
                ins.then_inc(s_hf, 1)
                dve.wait_ge(s_hf, k + 1)
                nc.vector.tensor_copy(h_hi[:], hT[:]).then_inc(s_hi, 1)
                dve.wait_ge(s_hi, k + 1)
                nc.vector.tensor_tensor(h_lo[:], hT[:], h_hi[:].bitcast(F32), ALU.subtract).then_inc(s_h, 1)

            def gated(k, c):
                dve.wait_ge(s_gate, k * FB + (c + 1))
                nc.vector.scalar_tensor_tensor(out=hid[:, c, :], in0=fps[c % 2][:, GT:2 * GT], scalar=b1[:, c:c + 1],
                                               in1=gate[:, c % 2, :], op0=ALU.add, op1=ALU.mult).then_inc(s_hid, 1)

            def after_feed_forward(k, u):
                dve.wait_ge(s_ff, k + 1)
                dve.wait_ge(s_yb, k + 1)
                yk = y[:, bass.ds(k * 2, 2), :]
                nc.vector.tensor_tensor(yk, fps[0][:, 0:2 * D].rearrange("p (t d) -> p t d", d=D), yk, ALU.add).then_inc(s_y, 1)
                dve.wait_ge(s_y, k + 1)
                dve.wait_ge(s_x[u], landed(k, u))
                nc.vector.tensor_tensor(x[u][:], x[u][:], yk, ALU.add).then_inc(s_xy, 1)
                dve.wait_ge(s_xy, k + 1)
                for t in range(2):
                    ins = nc.vector.bn_stats(xstats[:, t, :], x[u][:, t, :])
                ins.then_inc(s_xs, 1)
                dve.wait_ge(s_xs, 1)
                dve.wait_ge(s_xs, k + 1)
                for t in range(2):
                    ins = nc.vector.bn_aggr(xmv[:, t, :], xstats[:, t, :])
                ins.then_inc(s_xa, 1)
                dve.wait_ge(s_xa, k + 1)
                nc.vector.tensor_scalar(xvar[:], xmv[:, :, 1], EPS, None, ALU.add).then_inc(s_xv, 1)

            def normalised_x(k, u):
                dve.wait_ge(s_xr, k + 1)
                for t in range(2):
                    ins = nc.vector.tensor_scalar(xn[:, t, :], x[u][:, t, :], xmv[:, t, 0:1], xrstd[:, t:t + 1],
                                                  ALU.subtract, ALU.mult)
                ins.then_inc(s_xn, 1)

            def transposed_x(k, u):
                dve.wait_ge(s_xps, k + 1)
                nc.vector.tensor_copy(xT[u][:], xps[:, 0:GT]).then_inc(s_xf, 1)
                dve.wait_ge(s_xf, k + 1)
                nc.vector.tensor_copy(x_hi[u][:], xT[u][:]).then_inc(s_xhi, 1)
                dve.wait_ge(s_xhi, k + 1)
                nc.vector.tensor_tensor(x_lo[u][:], xT[u][:], x_hi[u][:].bitcast(F32), ALU.subtract).then_inc(s_xT, 1)

            def route(k, u):
                dve.wait_ge(s_lg, k + 1)
                nc.vector.tensor_copy(logits[:], xps[:, GT:GT + 2 * E].rearrange("p (t e) -> p t e", e=E)).then_inc(s_lgs, 1)
                dve.wait_ge(s_lgs, 1)
                dve.wait_ge(s_lgs, k + 1)
                for t in range(2):
                    ins = nc.vector.max(best[:, t, :], logits[:, t, :])
                ins.then_inc(s_best, 1)
                dve.wait_ge(s_best, 1)
                dve.wait_ge(s_best, k + 1)
                for t in range(2):
                    nc.vector.max_index(place[:, t, :], best[:, t, :], logits[:, t, :])
                nc.vector.tensor_tensor(diff[:], best[:, :, 1], best[:, :, 0], ALU.subtract).then_inc(s_place, 1)

            def mixture(k, u):
                dve.wait_ge(s_place, k + 1)
                nc.vector.tensor_copy(placef[:], place[:, :, 0:2])
                dve.wait_ge(s_ratio, k + 1)
                nc.vector.tensor_scalar(denom[:], ratio[:], 1.0, None, ALU.add).then_inc(s_soft, 1)
                dve.wait_ge(s_soft, k * 4 + 1)
                nc.vector.reciprocal(p1[:], denom[:]).then_inc(s_soft, 1)
                dve.wait_ge(s_soft, k * 4 + 2)
                nc.vector.tensor_tensor(p2[:], p1[:], ratio[:], ALU.mult).then_inc(s_soft, 1)
                dve.wait_ge(s_soft, k * 4 + 3)
                for t in range(2):
                    ins = nc.vector.tensor_scalar(second[:, t, :], iota[:], placef[:, t, 1:2], p2[:, t:t + 1],
                                                  ALU.is_equal, ALU.mult)
                    ins = nc.vector.tensor_scalar(mix[u][:, t, :], iota[:], placef[:, t, 0:1], p1[:, t:t + 1],
                                                  ALU.is_equal, ALU.mult)
                ins.then_inc(s_soft, 1)
                dve.wait_ge(s_soft, k * 4 + 4)
                nc.vector.tensor_tensor(mix[u][:], mix[u][:], second[:], ALU.add).then_inc(s_mix, 1)

            def add_experts(g, u, half):
                if half == 0:
                    dve.wait_ge(s_mix, g + 1)
                for i in range(OB):
                    for t in range(2):
                        e = OB * half + i
                        n = 2 * e + t
                        if i == 0:
                            dve.wait_ge(s_eo, g * O_JOBS + (2 * half + t + 1))
                        if e > 0:
                            dve.wait_ge(s_acc, g * 2 * E + (n - 1))
                        xt = x[u][:, t, :]
                        nc.vector.scalar_tensor_tensor(out=xt, in0=ops[t][:, D * i:D * i + D], scalar=mix[u][:, t, e:e + 1],
                                                       in1=xt, op0=ALU.mult, op1=ALU.add).then_inc(s_acc, 1)

            statistics(0)
            normalised(0, 0)
            statistics(1)
            modulate(0)
            normalised(1, 1)

            def body(g, u):
                static = isinstance(g, int)
                now = not (static and g < 0)
                ahead = not (static and g >= NG - 1)
                stats_ahead = not (static and (g < 0 or g >= NG - 2))
                if stats_ahead:
                    statistics(g + 2)
                if ahead:
                    for c in range(FB):
                        gated(g + 1, c)
                if stats_ahead:
                    normalised(g + 2, u)
                if now:
                    add_experts(g, u, 0)
                if ahead:
                    after_feed_forward(g + 1, 1 - u)
                if not (static and g >= NG - 2):
                    modulate(g + 2)
                if ahead:
                    normalised_x(g + 1, 1 - u)
                    transposed_x(g + 1, 1 - u)
                    route(g + 1, 1 - u)
                if now:
                    add_experts(g, u, 1)
                if ahead:
                    mixture(g + 1, 1 - u)
            steps(dve, body)

        @block.tensor
        def _(pe):
            def transpose_tokens(k, u):
                pe.wait_ge(s_z, k + 1)
                if not (isinstance(k, int) and k == 0):
                    pe.wait_ge(s_hf, k)
                for t in range(2):
                    ins = nc.tensor.transpose(tps[:, P * t:P * t + P], z[u][:, t, :], ident[:])
                ins.then_inc(s_tps, 1)

            def hidden(k):
                pe.wait_ge(s_h, k + 1)
                for c in range(FB):
                    if isinstance(k, int) and k == 0 and c < 2:
                        pass
                    elif c == 0:
                        pe.wait_ge(s_y, k)
                    else:
                        pe.wait_ge(s_hid, k * FB + (c - 1))
                    for i, w in enumerate((FB + c, c)):
                        o = fps[c % 2][:, GT * i:GT * i + GT]
                        nc.tensor.matmul(o, w1_hi[:, P * w:P * w + P], h_hi[:], start=True, stop=False)
                        nc.tensor.matmul(o, w1_hi[:, P * w:P * w + P], h_lo[:], start=False, stop=False)
                        ins = nc.tensor.matmul(o, w1_lo[:, P * w:P * w + P], h_hi[:], start=False, stop=True)
                    ins.then_inc(s_u, 1)

            def feed_forward_out(k):
                pe.wait_ge(s_hid, k * FB + FB)
                for t in range(2):
                    for c in range(FB):
                        ins = nc.tensor.matmul(fps[0][:, D * t:D * t + D], hid[:, c, P * t:P * t + P], w2[:, c, :],
                                               start=c == 0, stop=c == FB - 1)
                ins.then_inc(s_ff, 1)

            def transpose_x(k, u):
                pe.wait_ge(s_xn, k + 1)
                for t in range(2):
                    ins = nc.tensor.transpose(xps[:, P * t:P * t + P], xn[:, t, :], ident[:])
                ins.then_inc(s_xps, 1)

            def router_logits(k, u):
                pe.wait_ge(s_xT, k + 1)
                for t in range(2):
                    ins = nc.tensor.matmul(xps[:, GT + E * t:GT + E * t + E], xT[u][:, P * t:P * t + P], routerT,
                                           start=True, stop=True)
                ins.then_inc(s_lg, 1)

            def expert_hidden(g, u, e):
                if not (isinstance(g, int) and g == 0 and e < 2):
                    pe.wait_ge(s_eg, g * E + (e - 1))
                for c in range(EB):
                    o = hps[e % 2][:, GT * c:GT * c + GT]
                    nc.tensor.matmul(o, e1_hi[:, e, P * c:P * c + P], x_hi[u][:], start=True, stop=False)
                    nc.tensor.matmul(o, e1_hi[:, e, P * c:P * c + P], x_lo[u][:], start=False, stop=False)
                    ins = nc.tensor.matmul(o, e1_lo[:, e, P * c:P * c + P], x_hi[u][:], start=False, stop=True)
                ins.then_inc(s_eh, 1)

            def expert_out(g, half):
                for t in range(2):
                    n = 2 * OB * half + t
                    if half:
                        pe.wait_ge(s_acc, g * 2 * E + (2 * OB * (half - 1) + 2 * OB - 1 + t))
                    elif not (isinstance(g, int) and g == 0):
                        pe.wait_ge(s_acc, g * 2 * E + (t - 1))
                    for i in range(OB):
                        e = OB * half + i
                        if t == 0:
                            pe.wait_ge(s_eg, g * E + (e + 1))
                        for c in range(EB):
                            ins = nc.tensor.matmul(ops[t][:, D * i:D * i + D], eh[e][:, c, P * t:P * t + P], e2[:, e, c, :],
                                                   start=c == 0, stop=c == EB - 1)
                    ins.then_inc(s_eo, 1)

            pe.wait_ge(s_w, 16 * 6)
            nc.tensor.transpose(xps[:, 0:E + 2 * FB], rows[:], ident[0:E + 2 * FB, 0:E + 2 * FB]).then_inc(s_rt, 1)
            transpose_tokens(0, 0)
            pe.wait_ge(s_wr, 3)

            def body(g, u):
                static = isinstance(g, int)
                now = not (static and g < 0)
                ahead = not (static and g >= NG - 1)
                if ahead:
                    hidden(g + 1)
                if now:
                    for e in range(OB):
                        expert_hidden(g, u, e)
                    expert_out(g, 0)
                if ahead:
                    feed_forward_out(g + 1)
                if not (static and g >= NG - 2):
                    transpose_tokens(g + 2, u)
                if now:
                    for e in range(OB, E):
                        expert_hidden(g, u, e)
                if ahead:
                    transpose_x(g + 1, 1 - u)
                if now:
                    expert_out(g, 1)
                if ahead:
                    router_logits(g + 1, 1 - u)
            steps(pe, body)


def build(nc, inputs, out):
    BATCH, S, D = inputs["x"].shape
    INNER = inputs["attn1_wq"].shape[1]
    E, _, F = inputs["e_w1"].shape
    T = BATCH * S
    sizes = dict(S=S, D=D, BATCH=BATCH, H=INNER // 64, NG=T // (4 * S), E=E, F=F, DFF=inputs["ff_w2"].shape[0])
    inputs = dict(inputs)
    tiles = "(t two) s d -> t (two s) d"
    inputs["x"] = inputs["x"].rearrange(tiles, two=2)
    context = inputs["context"].rearrange(tiles, two=2)
    out = out.rearrange(tiles, two=2)
    H, NT = sizes["H"], T // P

    with ExitStack() as ctx:
        def sb(n, shape, dt=F32):
            return ctx.enter_context(nc.sbuf_tensor(n, shape, dt))

        mem = dict(
            y=sb("y", [P, NT, D]),
            scale=sb("scale", [D, 3, BATCH]),
            shift=sb("shift", [D, 3, BATCH]),
            bias=sb("bias", [P, 3 * D]),
            ident=sb("ident", [P, P]),
            neg_half=sb("neg_half", [P, NT]),
        )
        with ExitStack() as products:
            def sbp(n, shape, dt=F32):
                return products.enter_context(nc.sbuf_tensor(n, shape, dt))
            mem["attn"] = [(sbp(f"A_hi{a}", [D, H, D], F32R), sbp(f"A_lo{a}", [D, H, D], F32R),
                            sbp(f"B{a}", [D, 2, H // 2, D])) for a in range(2)]
            setup_phase(nc, sizes, mem, inputs)
            for a in range(2):
                attention_phase(nc, f"attn{a + 1}", sizes, mem, a, mem["attn"][a],
                                mem["bias"][:, D * a:D * a + D], context if a else None)
        feed_forward_phase(nc, sizes, mem, inputs, out)


_INS = ["x", "cond_1024", "ctx_1024"] + [f"L0_xcond_{n}" for n in (
    "attn1_wq", "attn1_wk", "attn1_wv", "attn1_wo", "attn1_bo", "attn2_wq", "attn2_wk", "attn2_wv", "attn2_wo",
    "attn2_bo", "ff_w1", "ff_b1", "ff_w2", "ff_b2", "norm1_w", "norm1_b", "norm2_w", "norm2_b", "norm3_w",
    "norm3_b")] + ["L0_ffn_router_w", "L0_ffn_w1", "L0_ffn_w2"]
_NAMES = {"cond_1024": "cond", "ctx_1024": "context", "L0_ffn_router_w": "router_w", "L0_ffn_w1": "e_w1",
          "L0_ffn_w2": "e_w2"}


def kernel(**inputs):
    import numpy as _np
    import concourse.bacc as _bacc
    from concourse import mybir as _mybir
    from concourse.bass_utils import run_bass_kernel_spmd as _run

    nc = _bacc.Bacc("TRN2", target_bir_lowering=False, num_devices=1)
    arrays, aps = {}, {}
    for name in _INS:
        a = _np.ascontiguousarray(inputs[name])
        arrays[f"in_{name}"] = a
        short = _NAMES.get(name, name.replace("L0_xcond_", ""))
        aps[short] = nc.dram_tensor(f"in_{name}", a.shape, _mybir.dt.from_np(a.dtype), kind="ExternalInput").ap()
    out = nc.dram_tensor("out", inputs["x"].shape, F32, kind="ExternalOutput").ap()
    build(nc, aps, out)
    r = _run(nc, [arrays], core_ids=[0])
    return r.results[0]["out"]
```

```python
from contextlib import ExitStack

import concourse.bass as bass
from concourse import mybir

F32 = mybir.dt.float32
F32R = mybir.dt.float32r
U32 = mybir.dt.uint32
ALU = mybir.AluOpType
ACT = mybir.ActivationFunctionType
AX_X = mybir.AxisListType.X

P = 128
BANK = 512
RING = 4
EPS = 1e-5


def landed(k, u):
    return (k - u) * 8 + 16


class Intake:

    def __init__(self, nc, ctx, name, sizes, mem, norm, bias, before, context=None, swaps=True):
        def sem(n):
            return ctx.enter_context(nc.semaphore(f"{name}_{n}"))

        self.nc, self.mem, self.norm, self.bias, self.before, self.context = nc, mem, norm, bias, before, context
        self.swaps = swaps
        self.S, self.D, self.GT, self.NB, self.NG = sizes["S"], sizes["D"], 4 * sizes["S"], 4, sizes["NG"]
        self.z, self.hT = mem["z"], mem["hT"]
        self.sT = mem["sT"] if context is not None else mem["hT"]
        self.s_ctx = [sem(f"ctx_loaded{u}") for u in range(2)]
        self.s_stats0 = sem("stats0")
        self.s_stats = sem("stats")
        self.s_aggr = sem("aggr")
        self.s_var = sem("var")
        self.s_rstd = sem("rstd")
        self.s_z = sem("z")
        self.s_yb = sem("y_bias")
        self.s_tps = sem("tps")
        self.s_hf = sem("hf")
        self.s_hi = sem("hi")
        self.s_h = sem("h")
        self.s_swap = sem("swap")

    def load_context(self, sp, k, u):
        sp.dma_start(self.mem["c_in"][u][:],
                     self.context[bass.ds(k * 2, 2)].rearrange("t p d -> p t d")).then_inc(self.s_ctx[u], 16)

    def statistics(self, dve, k):
        nc, y, stats, mv = self.nc, self.mem["y"], self.mem["stats"], self.mem["mv"]
        for t in range(2):
            ins = nc.vector.bn_stats(stats[:, t, :], y[:, bass.ds(k * 2 + t, 1), :])
        if isinstance(k, int) and k == 0:
            ins.then_inc(self.s_stats0, 1)
            dve.wait_ge(self.s_stats0, 1)
        else:
            ins.then_inc(self.s_stats, 1)
            dve.wait_ge(self.s_stats, 1)
            dve.wait_ge(self.s_stats, k)
        for t in range(2):
            ins = nc.vector.bn_aggr(mv[:, t, :], stats[:, t, :])
        ins.then_inc(self.s_aggr, 1)
        dve.wait_ge(self.s_aggr, k + 1)
        nc.vector.tensor_scalar(self.mem["var"][:], mv[:, :, 1], EPS, None, ALU.add).then_inc(self.s_var, 1)

    def rstd(self, pool, k):
        pool.wait_ge(self.s_var, k + 1)
        self.nc.gpsimd.tensor_tensor(self.mem["rstd"][:], self.mem["var"][:], self.mem["neg_half"][:, 0:2],
                                     ALU.pow).then_inc(self.s_rstd, 1)

    def normalised(self, dve, k, u):
        nc, y, mv = self.nc, self.mem["y"], self.mem["mv"]
        dve.wait_ge(self.s_rstd, k + 1)
        for t in range(2):
            ins = nc.vector.tensor_scalar(self.z[u][:, t:t + 1, :], y[:, bass.ds(k * 2 + t, 1), :], mv[:, t, 0:1],
                                          self.mem["rstd"][:, t:t + 1], ALU.subtract, ALU.mult)
        ins.then_inc(self.s_z, 1)
        dve.wait_ge(self.s_z, k + 1)
        yk = y[:, bass.ds(k * 2, 2), :]
        nc.vector.tensor_tensor(yk, yk, self.bias.unsqueeze(1).to_broadcast([P, 2, self.D]), ALU.add).then_inc(self.s_yb, 1)

    def transpose_tokens(self, pe, k, u):
        nc, tps, ident, GT = self.nc, self.mem["tps"], self.mem["ident"], self.GT
        pe.wait_ge(self.s_z, k + 1)
        if self.context is not None:
            pe.wait_ge(self.s_ctx[u], landed(k, u))
        if not (isinstance(k, int) and k == 0):
            pe.wait_ge(self.s_hf, k)
        elif self.before is not None:
            pe.wait_ge(self.before.s_hf, self.NG)
        for t in range(2):
            ins = nc.tensor.transpose(tps[:, P * t:P * t + P], self.z[u][:, t, :], ident[:])
        if self.context is not None:
            for t in range(2):
                ins = nc.tensor.transpose(tps[:, GT + P * t:GT + P * t + P], self.mem["c_in"][u][:, t, :], ident[:])
        ins.then_inc(self.s_tps, 1)

    def modulate(self, dve, k, u):
        nc, tps, S, NB, hT, sT = self.nc, self.mem["tps"], self.S, self.NB, self.hT[u], self.sT[u]
        s_hi, s_lo = self.mem["s_hi"][u], self.mem["s_lo"][u]
        dve.wait_ge(self.s_tps, k + 1)
        if self.context is not None:
            nc.vector.tensor_copy(sT[:], tps[:, self.GT:2 * self.GT])
        for b in range(NB):
            ins = nc.vector.tensor_scalar(hT[:, S * b:S * b + S], tps[:, S * b:S * b + S],
                                          self.mem["scale"][:, self.norm, bass.ds(k * NB + b, 1)],
                                          self.mem["shift"][:, self.norm, bass.ds(k * NB + b, 1)], ALU.mult, ALU.add)
        ins.then_inc(self.s_hf, 1)
        dve.wait_ge(self.s_hf, k + 1)
        nc.vector.tensor_copy(s_hi[:], sT[:]).then_inc(self.s_hi, 1)
        dve.wait_ge(self.s_hi, k + 1)
        nc.vector.tensor_tensor(s_lo[:], sT[:], s_hi[:].bitcast(F32), ALU.subtract).then_inc(self.s_h, 1)

    def swap(self, pool, k, u):
        nc, w_hi, w_lo = self.nc, self.mem["w_hi"][u], self.mem["w_lo"][u]
        pool.wait_ge(self.s_h, k + 1)
        whole, high = (a.rearrange("d (p b k) -> d p b k", p=2, b=2)
                       for a in (self.sT[u][:], self.mem["s_hi"][u][:].bitcast(F32)))
        for b in range(2):
            nc.gpsimd.tensor_tensor(w_lo[:, :, b, :], whole[:, :, 1 - b, :], high[:, :, 1 - b, :], ALU.subtract)
        for b in range(2):
            ins = nc.gpsimd.tensor_copy(w_hi[:, :, b, :], high[:, :, 1 - b, :])
        ins.then_inc(self.s_swap, 1)


def attention_phase(nc, name, sizes, mem, intake, weights, following, side_work=None):
    S, D, H, NG = sizes["S"], sizes["D"], sizes["H"], sizes["NG"]
    GT, NB, NP = 4 * S, 4, 2
    HC = BANK // S
    QC = BANK // D
    A_hi, A_lo, B_hi, B_lo = weights
    y, ident, hT, s_hi_buf, s_lo_buf = mem["y"], mem["ident"], intake.hT, mem["s_hi"], mem["s_lo"]
    G_JOBS, T_JOBS, V_JOBS = H * GT // BANK, H // 2 // QC, 2 * (H // 2) // QC
    JOBS = G_JOBS + 2 * T_JOBS + 2 * V_JOBS

    with ExitStack() as ctx:
        def sb(n, shape, dt=F32):
            return ctx.enter_context(nc.sbuf_tensor(f"{name}_{n}", shape, dt))

        def ps(n, shape):
            return ctx.enter_context(nc.psum_tensor(f"{name}_{n}", shape, F32))

        def sem(n):
            return ctx.enter_context(nc.semaphore(f"{name}_{n}"))

        G = sb("G", [D, H // 2, 4, NP, S])
        V = [sb(f"V{u}", [P, NB, H // 2, D]) for u in range(2)]
        Pr = [[sb(f"P{u}{p}", [P, H, S]) for p in range(NP)] for u in range(2)]
        PT = sb("PT", [P, NP, H // 2, P])
        top = sb("top", [P, H])
        total = sb("total", [P, H])
        inv = [sb(f"inv{p}", [P, H]) for p in range(NP)]

        ring = [ps(f"ring{i}", [P, BANK]) for i in range(RING)]
        Sps = ps("S", [P, 2 * BANK])
        ops = ps("ops", [P, BANK])

        s_full = sem("ring_full")
        s_free = sem("ring_free")
        s_S = sem("scores")
        s_top = sem("top")
        s_sub = sem("sub")
        s_exp = sem("exp")
        s_sum = sem("sum")
        s_inv = sem("inv")
        s_P = sem("P")
        s_o = sem("o")
        s_y = sem("y")

        block = ctx.enter_context(nc.Block())

        def turn(step, local):
            return local if isinstance(step, int) and step == 0 else step * JOBS + (local - 2 * T_JOBS)

        def locals_of(step):
            if isinstance(step, int) and step == 0:
                return [G_JOBS, G_JOBS + V_JOBS], None
            if isinstance(step, int) and step == NG:
                return None, [0, T_JOBS]
            t0 = G_JOBS
            return [t0 + T_JOBS, t0 + 2 * T_JOBS + V_JOBS], [t0, t0 + T_JOBS + V_JOBS]

        def steps(eng, body):
            body(0, 0)
            with eng.Fori(0, NG - 5, 2) as i:
                body(i + 1, 1)
                body(i + 2, 0)
            for g in range(NG - 3, NG + 1):
                body(g, g % 2)

        @block.sync
        def _(sp):
            if following.context is not None:
                following.load_context(sp, 0, 0)
                following.load_context(sp, 1, 1)
            if side_work is not None:
                side_work[0](sp)
            if intake.context is not None:
                def later(k, u):
                    sp.wait_ge(intake.s_tps, k - 1)
                    intake.load_context(sp, k, u)
                with sp.Fori(0, NG - 3, 2) as i:
                    later(i + 2, 0)
                    later(i + 3, 1)

        @block.gpsimd
        def _(pool):
            def normalise(g, u, p):
                pool.wait_ge(s_inv, g * 2 + (p + 1))
                pr = Pr[u][p]
                nc.gpsimd.tensor_tensor(pr[:], pr[:], inv[p][:].unsqueeze(2).to_broadcast([P, H, S]),
                                        ALU.mult).then_inc(s_P, 1)

            def body(g, u):
                static = isinstance(g, int)
                now = not (static and g == NG)
                hand_over = static and g == NG - 1
                if not (static and g >= NG - 2):
                    intake.rstd(pool, g + 2)
                if hand_over:
                    following.rstd(pool, 0)
                if now:
                    normalise(g, u, 0)
                if not (static and g >= NG - 1):
                    intake.swap(pool, g + 1, 1 - u)
                if hand_over:
                    following.rstd(pool, 1)
                if now:
                    normalise(g, u, 1)
                if hand_over and following.swaps:
                    following.swap(pool, 0, 0)
                if static and side_work is not None:
                    side_work[1](pool, g)
            steps(pool, body)

        @block.scalar
        def _(act):
            def copy_out(step, local, out):
                n = turn(step, local)
                act.wait_ge(s_full, n + 1)
                src = ring[local % RING][:]
                nc.scalar.copy(out, src).then_inc(s_free, 1)

            def exps(g, u, p):
                act.wait_ge(s_sub, g * 2 + (p + 1))
                nc.scalar.activation(Pr[u][p][:], Pr[u][p][:], ACT.Exp).then_inc(s_exp, 1)

            def body(g, u):
                last = isinstance(g, int) and g == NG
                values, transposed = locals_of(g)
                if not last:
                    for j in range(G_JOBS):
                        copy_out(g, j, G[:, j, :, :, :])
                for p in range(NP):
                    if transposed:
                        for c in range(T_JOBS):
                            copy_out(g, transposed[p] + c, PT[:, p, QC * c:QC * c + QC, :])
                    if not last:
                        for i in range(V_JOBS):
                            if i == V_JOBS - 1:
                                exps(g, u, p)
                            c, par = i // 2, i % 2
                            n = turn(g, values[p] + i)
                            act.wait_ge(s_full, n + 1)
                            for half in range(2):
                                rows, b = slice(S * half, S * half + S), half ^ par
                                ins = nc.scalar.copy(V[u][rows, 2 * p + b, QC * c:QC * c + QC, :],
                                                     ring[(values[p] + i) % RING][rows, :])
                            ins.then_inc(s_free, 1)
            steps(act, body)

        @block.vector
        def _(dve):
            def subtract_max(g, u, p):
                dve.wait_ge(s_S, g * 2 + (p + 1))
                sc = Sps[:].rearrange("q (h k) -> q h k", k=S)
                nc.vector.tensor_reduce(top[:], sc, AX_X, ALU.max).then_inc(s_top, 1)
                dve.wait_ge(s_top, g * 2 + (p + 1))
                nc.vector.tensor_tensor(Pr[u][p][:], sc, top[:].unsqueeze(2).to_broadcast([P, H, S]),
                                        ALU.subtract).then_inc(s_sub, 1)

            def sums(g, u, p):
                dve.wait_ge(s_exp, g * 2 + (p + 1))
                nc.vector.tensor_reduce(total[:], Pr[u][p][:], AX_X, ALU.add).then_inc(s_sum, 1)
                dve.wait_ge(s_sum, g * 2 + (p + 1))
                nc.vector.reciprocal(inv[p][:], total[:]).then_inc(s_inv, 1)

            def residual(g, p):
                dve.wait_ge(s_o, g * 2 + (p + 1))
                if p == 0:
                    dve.wait_ge(intake.s_yb, g + 1)
                yt = y[:, bass.ds(g * 2 + p, 1), :]
                nc.vector.tensor_tensor(yt, ops[:, 0:D].unsqueeze(1), yt, ALU.add).then_inc(s_y, 1)

            def body(g, u):
                static = isinstance(g, int)
                ahead2 = not (static and g >= NG - 2)
                ahead1 = not (static and g >= NG - 1)
                now = not (static and g >= NG)
                behind = not (static and g == 0)
                hand_over = static and g == NG - 1
                if ahead2:
                    intake.statistics(dve, g + 2)
                if hand_over:
                    dve.wait_ge(s_y, 4)
                    following.statistics(dve, 0)
                if now:
                    subtract_max(g, u, 0)
                if behind:
                    residual(g - 1, 0)
                if now:
                    sums(g, u, 0)
                if not behind:
                    intake.modulate(dve, g + 1, 1 - u)
                if now:
                    subtract_max(g, u, 1)
                if ahead1 and behind:
                    intake.modulate(dve, g + 1, 1 - u)
                if ahead2:
                    intake.normalised(dve, g + 2, u)
                if hand_over:
                    following.normalised(dve, 0, 0)
                    following.statistics(dve, 1)
                if now:
                    sums(g, u, 1)
                if behind:
                    residual(g - 1, 1)
                if hand_over:
                    following.modulate(dve, 0, 0)
                    following.normalised(dve, 1, 1)
            steps(dve, body)

        @block.tensor
        def _(pe):
            def turned(step, local):
                n = turn(step, local)
                if not (isinstance(n, int) and n < RING):
                    pe.wait_ge(s_free, n - (RING - 1))
                return ring[local % RING]

            def keys(g, u):
                pe.wait_ge(intake.s_h, g + 1)
                for j in range(G_JOBS):
                    bank = turned(g, j)
                    places = bank[:].rearrange("d (q p k) -> d p q k", p=NP, k=S)
                    for i in range(2):
                        out, h = places[:, :, slice(0, 4, 3) if i == 0 else slice(1, 3), :], 2 * j + i
                        nc.tensor.matmul(out, A_hi[:, h, :], s_hi_buf[u][:], start=True, stop=False)
                        nc.tensor.matmul(out, A_hi[:, h, :], s_lo_buf[u][:], start=False, stop=False)
                        ins = nc.tensor.matmul(out, A_lo[:, h, :], s_hi_buf[u][:], start=False, stop=True)
                    ins.then_inc(s_full, 1)

            def scores(g, u, p):
                pe.wait_ge(s_free, turn(g, G_JOBS))
                if not (isinstance(g, int) and g == 0 and p == 0):
                    pe.wait_ge(s_sub, g * 2 + p)
                for c in range(H // HC):
                    bank = Sps[:, BANK * c:BANK * c + BANK]
                    for b in range(2):
                        tok = S * (2 * p + b)
                        ins = nc.tensor.matmul(bank[S * b:S * b + S, :], hT[u][:, tok:tok + S],
                                               G[:, HC // 2 * c:HC // 2 * c + HC // 2, 2 * b:2 * b + 2, p, :],
                                               start=True, stop=True)
                ins.then_inc(s_S, 1)

            def values(g, u, p, local):
                if p == 0:
                    pe.wait_ge(intake.s_swap, g + 1)
                for i in range(V_JOBS):
                    c, par = i // 2, i % 2
                    bank = turned(g, local + i)
                    if par:
                        hi, lo = (w[u][:, p, :, :].rearrange("d b k -> d (b k)") for w in (mem["w_hi"], mem["w_lo"]))
                    else:
                        hi, lo = (w[u][:, P * p:P * p + P] for w in (s_hi_buf, s_lo_buf))
                    cols = slice(QC * c, QC * c + QC)
                    nc.tensor.matmul(bank[:], hi, B_hi[:, par, cols, :], start=True, stop=False)
                    nc.tensor.matmul(bank[:], lo, B_hi[:, par, cols, :], start=False, stop=False)
                    ins = nc.tensor.matmul(bank[:], hi, B_lo[:, par, cols, :], start=False, stop=True)
                    ins.then_inc(s_full, 1)

            def transpose_probabilities(g, u, p, step, local):
                pe.wait_ge(s_P, g * 2 + (p + 1))
                pr = Pr[u][p][:].rearrange("q h k -> q (h k)")
                for c in range(T_JOBS):
                    bank = turned(step, local + c)
                    for i in range(QC):
                        n = QC * c + i
                        ins = nc.tensor.transpose(bank[:, P * i:P * i + P], pr[:, P * n:P * n + P], ident[:])
                    ins.then_inc(s_full, 1)

            def weighted_sum(g, u, p, step, local):
                pe.wait_ge(s_free, turn(step, local + T_JOBS))
                if not (isinstance(g, int) and g == 0 and p == 0):
                    pe.wait_ge(s_y, g * 2 + p)
                for n in range(H // 2):
                    for b in range(2):
                        ins = nc.tensor.matmul(ops[S * b:S * b + S, 0:D], PT[:, p, n, S * b:S * b + S],
                                               V[u][:, 2 * p + b, n, :], start=n == 0, stop=n == H // 2 - 1)
                ins.then_inc(s_o, 1)

            def body(g, u):
                static = isinstance(g, int)
                now = not (static and g >= NG)
                ahead = not (static and g >= NG - 1)
                vl, tl = locals_of(g)
                if now:
                    keys(g, u)
                if tl:
                    transpose_probabilities(g - 1, 1 - u, 0, g, tl[0])
                if now:
                    scores(g, u, 0)
                    values(g, u, 0, vl[0])
                if tl:
                    weighted_sum(g - 1, 1 - u, 0, g, tl[0])
                    transpose_probabilities(g - 1, 1 - u, 1, g, tl[1])
                if not tl:
                    intake.transpose_tokens(pe, g + 1, 1 - u)
                if now:
                    scores(g, u, 1)
                if ahead and tl:
                    intake.transpose_tokens(pe, g + 1, 1 - u)
                if now:
                    values(g, u, 1, vl[1])
                if tl:
                    weighted_sum(g - 1, 1 - u, 1, g, tl[1])
                if static and g == NG - 1:
                    following.transpose_tokens(pe, 0, 0)
            steps(pe, body)


def setup_phase(nc, sizes, mem, inputs, following):
    S, D, H, NG, BATCH = sizes["S"], sizes["D"], sizes["H"], sizes["NG"], sizes["BATCH"]
    HP = H // 2
    NT = 2 * NG
    XC = 4
    dh = S
    y, scale, shift, ident = mem["y"], mem["scale"], mem["shift"], mem["ident"]

    with ExitStack() as ctx:
        def sb(n, shape, dt=F32):
            return ctx.enter_context(nc.sbuf_tensor(f"set_{n}", shape, dt))

        def sem(n):
            return ctx.enter_context(nc.semaphore(f"set_{n}"))

        x = sb("x", [P, NT, D])
        E = sizes["E"]
        NROW = BATCH + 6 + E + 2 * sizes["DFF"] // P
        rows = sb("rows", [NROW, D])
        rowsT = sb("rowsT", [D, BATCH + 6])
        nw = sb("nw", [D, 3, 2 * D])
        biases = sb("biases", [1, 3, D])
        ones = sb("ones", [1, P])
        w_in = [[sb(f"w{m}{a}", [D, H * dh]) for m in range(3)] for a in range(2)]
        wo = [sb(f"wo{a}", [P, HP, D]) for a in range(2)]
        wT = [sb(f"wT{m}", [P, HP, D]) for m in range(3)]
        stats = sb("stats", [P, NT, 6])
        mv = sb("mv", [P, NT, 2])
        var = sb("var", [P, NT])
        rstd = sb("rstd", [P, NT])
        ring = [ctx.enter_context(nc.psum_tensor(f"set_ring{i}", [P, BANK], F32)) for i in range(7)]
        misc, ring = ring[5:], ring[:5]
        NR = len(ring)

        s_x = [sem(f"x{i}") for i in range(XC)]
        s_cond0 = sem("cond_loaded")
        s_cond = sem("small_loaded")
        s_w = [[sem(f"w{m}{a}_loaded") for m in range(4)] for a in range(2)]
        s_ident = sem("ident")
        s_ones = sem("ones")
        s_half = sem("half")
        s_rowsT = sem("rowsT")
        s_cT = sem("cT")
        s_emb = sem("emb")
        s_bias = sem("bias")
        s_stats = sem("stats")
        s_aggr = sem("aggr")
        s_var = sem("var")
        s_rstd = sem("rstd")
        s_full = sem("full")
        s_free = sem("free")
        s_lo = sem("lo")
        s_y = sem("y")
        s_mod = sem("mod")
        block = ctx.enter_context(nc.Block())

        TB = HP * P // BANK
        AB = H * D // BANK
        PB = BANK // P
        TURNS = 3 * TB + 2 * AB
        FACTOR = (dh ** -0.5, 1.0)
        per = NT // XC

        def heads_of(a, product, low, i):
            par, c = i // (AB // 2), i % (AB // 2)
            w = mem["attn"][a][2 * product + low]
            if product:
                return w[:, par, PB * c:PB * c + PB, :]
            return w[:].rearrange("p (n two) d -> p n two d", two=2)[:, PB * c:PB * c + PB, par, :]

        def products_before(n):
            return sum(min(max(n - a * TURNS - 3 * TB, 0), 2 * AB) for a in range(2))

        @block.sync
        def _(sp):
            for a in range(2):
                for m, n in enumerate(("wq", "wk", "wv")):
                    sp.dma_start(w_in[a][m][:], inputs[f"attn{a + 1}_{n}"]).then_inc(s_w[a][m], 16)
                sp.dma_start(wo[a][:], inputs[f"attn{a + 1}_wo"].rearrange("(h p) d -> p h d", p=P)).then_inc(s_w[a][3], 16)

        @block.gpsimd
        def _(pool):
            nc.gpsimd.memset(ident[:], 0.0).then_inc(s_ident, 1)
            pool.wait_ge(s_ident, 1)
            nc.gpsimd.affine_select(out=ident[:], in_=ident[:], compare_op=ALU.not_equal, fill=1.0, base=0,
                                    pattern=[[-1, P]], channel_multiplier=1).then_inc(s_ident, 1)
            for i in range(3):
                pool.dma_start(nw[:, i, :], inputs[f"norm{i + 1}_w"]).then_inc(s_cond, 16)
                pool.dma_start(rows[BATCH + 2 * i:BATCH + 2 * i + 2, :],
                               inputs[f"norm{i + 1}_b"].rearrange("(c p) -> c p", p=D)).then_inc(s_cond, 16)
            for i, n in enumerate(("attn1_bo", "attn2_bo", "ff_b2")):
                pool.dma_start(biases[:, i, :], inputs[n].rearrange("(a n) -> a n", a=1)).then_inc(s_cond, 16)
            pool.dma_start(rows[BATCH + 6:BATCH + 6 + E, :], inputs["router_w"]).then_inc(s_cond, 16)
            pool.dma_start(rows[BATCH + 6 + E:, :], inputs["ff_b1"].rearrange("(c p) -> c p", p=P)).then_inc(s_cond, 16)
            nc.gpsimd.memset(ones[:], 1.0).then_inc(s_ones, 1)
            nc.gpsimd.memset(mem["neg_half"][:], -0.5).then_inc(s_half, 1)
            pool.wait_ge(s_half, 1)
            for i in range(XC):
                piece = slice(i * per, i * per + per)
                pool.wait_ge(s_var, i + 1)
                nc.gpsimd.tensor_tensor(rstd[:, piece], var[:, piece], mem["neg_half"][:, piece], ALU.pow).then_inc(s_rstd, 1)
            following.rstd(pool, 0)
            following.rstd(pool, 1)
            following.swap(pool, 0, 0)

        @block.scalar
        def _(act):
            act.dma_start(rows[0:BATCH, :], inputs["cond"]).then_inc(s_cond0, 16)
            for i in range(XC):
                act.dma_start(x[:, i * per:i * per + per, :],
                              inputs["x"][i * per:i * per + per].rearrange("t p d -> p t d")).then_inc(s_x[i], 16)
            for a in range(2):
                n = a * TURNS
                for m in range(3):
                    for c in range(TB):
                        act.wait_ge(s_full, n + 1)
                        nc.scalar.copy(wT[m][:, PB * c:PB * c + PB, :], ring[n % NR][:]).then_inc(s_free, 1)
                        n += 1
                for product in range(2):
                    for i in range(AB):
                        act.wait_ge(s_full, n + 1)
                        nc.scalar.activation(heads_of(a, product, 0, i), ring[n % NR][:].rearrange("p (n d) -> p n d", d=D),
                                             ACT.Copy, scale=FACTOR[product]).then_inc(s_free, 1)
                        n += 1

        @block.vector
        def _(dve):
            def statistics(i):
                piece = slice(i * per, i * per + per)
                dve.wait_ge(s_x[i], 16)
                for t in range(i * per, i * per + per):
                    nc.vector.bn_stats(stats[:, t, :], x[:, t, :]).then_inc(s_stats, 1)
                dve.wait_ge(s_stats, i * per + per)
                for t in range(i * per, i * per + per):
                    nc.vector.bn_aggr(mv[:, t, :], stats[:, t, :]).then_inc(s_aggr, 1)
                dve.wait_ge(s_aggr, i * per + per)
                nc.vector.tensor_scalar(var[:, piece], mv[:, piece, 1], EPS, None, ALU.add).then_inc(s_var, 1)

            def normalised(i):
                dve.wait_ge(s_rstd, i + 1)
                for t in range(i * per, i * per + per):
                    ins = nc.vector.tensor_scalar(y[:, t, :], x[:, t, :], mv[:, t, 0:1], rstd[:, t:t + 1],
                                                  ALU.subtract, ALU.mult)
                ins.then_inc(s_y, 1)

            def low_parts(a, product):
                for i in range(AB):
                    n = a * TURNS + 3 * TB + product * AB + i
                    dve.wait_ge(s_free, n + 1)
                    nc.vector.scalar_tensor_tensor(out=heads_of(a, product, 1, i),
                                                   in0=ring[n % NR][:].rearrange("p (n d) -> p n d", d=D),
                                                   scalar=FACTOR[product], in1=heads_of(a, product, 0, i).bitcast(F32),
                                                   op0=ALU.mult, op1=ALU.subtract).then_inc(s_lo, 1)

            statistics(0)
            statistics(1)
            low_parts(0, 0)
            normalised(0)
            statistics(2)
            low_parts(0, 1)
            normalised(1)
            statistics(3)
            dve.wait_ge(s_rowsT, 1)
            nc.vector.tensor_copy(mem["rowsT"][:], misc[0][:, BATCH + 6:NROW])
            nc.vector.tensor_copy(rowsT[:], misc[0][:, 0:BATCH + 6]).then_inc(s_cT, 1)
            normalised(2)
            normalised(3)
            dve.wait_ge(s_emb, 1)
            for i in range(3):
                nb = rowsT[:, BATCH + 2 * i:BATCH + 2 * i + 2]
                src = misc[1][:, 2 * BATCH * i:2 * BATCH * i + 2 * BATCH]
                nc.vector.tensor_scalar(scale[:, i, :], src[:, 0:BATCH], nb[:, 0:1], 1.0, ALU.add, ALU.add)
                nc.vector.tensor_scalar(shift[:, i, :], src[:, BATCH:], nb[:, 1:2], None, ALU.add)
            dve.wait_ge(s_bias, 1)
            nc.vector.tensor_copy(mem["bias"][:], misc[0][:, 0:3 * D]).then_inc(s_mod, 1)
            dve.wait_ge(s_y, 1)
            following.statistics(dve, 0)
            dve.wait_ge(s_mod, 1)
            following.normalised(dve, 0, 0)
            following.statistics(dve, 1)
            low_parts(1, 0)
            following.modulate(dve, 0, 0)
            following.normalised(dve, 1, 1)
            low_parts(1, 1)

        @block.tensor
        def _(pe):
            pe.wait_ge(s_ident, 2)

            def turned(n):
                if n >= NR:
                    pe.wait_ge(s_free, n - NR + 1)
                if products_before(n - NR + 1):
                    pe.wait_ge(s_lo, products_before(n - NR + 1))
                return ring[n % NR]

            for a in range(2):
                n = a * TURNS
                for m in range(3):
                    pe.wait_ge(s_w[a][m], 16)
                    for c in range(TB):
                        bank = turned(n)
                        for i in range(PB):
                            k = PB * c + i
                            ins = nc.tensor.transpose(bank[:, P * i:P * i + P], w_in[a][m][:, P * k:P * k + P], ident[:])
                        ins.then_inc(s_full, 1)
                        n += 1
                pe.wait_ge(s_free, n)
                pe.wait_ge(s_w[a][3], 16)
                if a == 1:
                    pe.wait_ge(s_cT, 1)
                    for i in range(3):
                        for c in range(2):
                            o = BATCH * (2 * i + c)
                            ins = nc.tensor.matmul(misc[1][:, o:o + BATCH], nw[:, i, D * c:D * c + D], rowsT[:, 0:BATCH],
                                                   start=True, stop=True)
                    ins.then_inc(s_emb, 1)
                    pe.wait_ge(s_ones, 1)
                    nc.tensor.matmul(misc[0][:, 0:3 * D], ones[:], biases[:].rearrange("a b d -> a (b d)"),
                                     start=True, stop=True).then_inc(s_bias, 1)
                for product, (left, right) in enumerate(((wT[1], wT[0]), (wT[2], wo[a]))):
                    for i in range(AB):
                        par, c = i // (AB // 2), i % (AB // 2)
                        half = slice(dh * par, dh * par + dh)
                        bank = turned(n)
                        for j in range(PB):
                            k = PB * c + j
                            ins = nc.tensor.matmul(bank[:, D * j:D * j + D], left[half, k, :], right[half, k, :],
                                                   start=True, stop=True)
                        ins.then_inc(s_full, 1)
                        n += 1
                    if a == 1 and product == 0:
                        following.transpose_tokens(pe, 0, 0)
                if a == 0:
                    pe.wait_ge(s_cond0, 16)
                    pe.wait_ge(s_cond, 16 * 11)
                    nc.tensor.transpose(misc[0][:, 0:NROW], rows[:], ident[0:NROW, 0:NROW]).then_inc(s_rowsT, 1)


def feed_forward_phase(nc, sizes, mem, intake, inputs, out):
    S, D, NG = sizes["S"], sizes["D"], sizes["NG"]
    E, F = sizes["E"], sizes["F"]
    DFF = sizes["DFF"]
    GT, NB = 4 * S, 4
    FB, EB = DFF // P, F // P
    y, ident, h_hi, h_lo = mem["y"], mem["ident"], mem["s_hi"], mem["s_lo"]

    with ExitStack() as ctx:
        def sb(n, shape, dt=F32):
            return ctx.enter_context(nc.sbuf_tensor(f"ff_{n}", shape, dt))

        def ps(n, shape):
            return ctx.enter_context(nc.psum_tensor(f"ff_{n}", shape, F32))

        def sem(n):
            return ctx.enter_context(nc.semaphore(f"ff_{n}"))

        w1_hi, w1_lo, w2, e2 = mem["w1_hi"], mem["w1_lo"], mem["w2"], mem["e2"]
        e1_hi, e1_lo = (mem[n][:].rearrange("d (e f) -> d e f", e=E) for n in ("e1_hi", "e1_lo"))
        routerT, b1 = mem["rowsT"][:, 0:E], mem["rowsT"][:, E:]
        iota = sb("iota", [P, E])
        euler = sb("euler", [P, 2])
        gate = sb("gate", [P, 2, GT])
        hid = sb("hid", [P, FB, GT])
        x = [sb(f"x{u}", [P, 2, D]) for u in range(2)]
        odd = sb("odd", [P, 2, D])
        xn = sb("xn", [P, 2, D])
        xT = [sb(f"xT{u}", [D, GT]) for u in range(2)]
        x_hi = [sb(f"x_hi{u}", [D, GT], F32R) for u in range(2)]
        x_lo = [sb(f"x_lo{u}", [D, GT], F32R) for u in range(2)]
        eh = [sb(f"eh{i}", [P, EB, GT]) for i in range(E)]
        xstats = sb("xstats", [P, 2, 6])
        xmv = sb("xmv", [P, 2, 2])
        xvar = sb("xvar", [P, 2])
        xrstd = sb("xrstd", [P, 2])
        logits = sb("logits", [P, 2, E])
        best = sb("best", [P, 2, 8])
        place = sb("place", [P, 2, 8], U32)
        placef = sb("placef", [P, 2, 2])
        diff = sb("diff", [P, 2])
        ratio = sb("ratio", [P, 2])
        denom = sb("denom", [P, 2])
        p1 = sb("p1", [P, 2])
        p2 = sb("p2", [P, 2])
        second = sb("second", [P, 2, E])
        mix = [sb(f"mix{u}", [P, 2, E]) for u in range(2)]

        xps = ps("xps", [P, BANK])
        fps = [ps(f"fps{i}", [P, BANK]) for i in range(2)]
        hps = [ps(f"hps{i}", [P, BANK]) for i in range(2)]
        ops = [ps(f"ops{i}", [P, BANK]) for i in range(2)]
        OB = BANK // D
        HALVES = E // OB
        ADDS = 2 * E + 2

        s_x = [sem(f"x_loaded{u}") for u in range(2)]
        s_const = sem("const")
        s_u = sem("u")
        s_gate = sem("gate")
        s_hid = sem("hid")
        s_ff = sem("ff")
        s_xy0 = sem("xy0")
        s_xy = sem("xy")
        s_xs = sem("xs")
        s_xa = sem("xa")
        s_xv = sem("xv")
        s_xr = sem("xr")
        s_xn = sem("xn")
        s_xps = sem("xps")
        s_xhi = sem("xhi")
        s_xT = sem("xT")
        s_lg = sem("lg")
        s_lgs = sem("lgs")
        s_best = sem("best")
        s_place = sem("place")
        s_ratio = sem("ratio")
        s_soft = sem("soft")
        s_mix = sem("mix")
        s_eh = sem("eh_psum")
        s_eg = sem("eh")
        s_eo = sem("eo")
        s_acc = sem("acc")
        s_out = [sem(f"out{u}") for u in range(2)]
        block = ctx.enter_context(nc.Block())

        def job_start(job):
            return job * OB + max(job - (2 * HALVES - 2), 0)

        def steps(eng, body):
            body(-1, 1)
            body(0, 0)
            with eng.Fori(0, NG - 5, 2) as i:
                body(i + 1, 1)
                body(i + 2, 0)
            for g in range(NG - 3, NG):
                body(g, g % 2)

        @block.sync
        def _(sp):
            def load(k, u):
                sp.dma_start(x[u][:], inputs["x"][bass.ds(k * 2, 2)].rearrange("t p d -> p t d")).then_inc(s_x[u], 16)

            load(0, 0)
            load(1, 1)

            def body(g, u):
                if isinstance(g, int) and g < 0:
                    return
                sp.wait_ge(s_acc, g * ADDS + ADDS)
                sp.dma_start(out[bass.ds(g * 2, 2)].rearrange("t p d -> p t d"), x[u][:]).then_inc(s_out[u], 16)
                if not (isinstance(g, int) and g >= NG - 2):
                    sp.wait_ge(s_out[u], landed(g, u))
                    load(g + 2, u)
            steps(sp, body)
            for u in range(2):
                sp.wait_ge(s_out[u], landed(NG - 2 + u, u))

        @block.gpsimd
        def _(pool):
            nc.gpsimd.iota(iota[:], [[1, E]], base=0, channel_multiplier=0,
                           allow_small_or_imprecise_dtypes=True).then_inc(s_const, 1)
            nc.gpsimd.memset(euler[:], 2.718281828459045).then_inc(s_const, 1)
            pool.wait_ge(s_const, 2)

            def body(g, u):
                if not (isinstance(g, int) and (g < 0 or g >= NG - 2)):
                    intake.rstd(pool, g + 2)
                if not (isinstance(g, int) and g >= NG - 1):
                    pool.wait_ge(s_xv, g + 2)
                    nc.gpsimd.tensor_tensor(xrstd[:], xvar[:], mem["neg_half"][:, 0:2], ALU.pow).then_inc(s_xr, 1)
                    pool.wait_ge(s_place, g + 2)
                    nc.gpsimd.tensor_tensor(ratio[:], euler[:], diff[:], ALU.pow).then_inc(s_ratio, 1)
            steps(pool, body)

        @block.scalar
        def _(act):
            def gates(k, c):
                act.wait_ge(s_u, k * FB + (c + 1))
                if not (isinstance(k, int) and k == 0 and c < 2):
                    act.wait_ge(s_hid, k * FB + (c - 1))
                nc.scalar.activation(gate[:, c % 2, :], fps[c % 2][:, 0:GT], ACT.Gelu,
                                     bias=b1[:, FB + c:FB + c + 1]).then_inc(s_gate, 1)

            def expert(g, e):
                act.wait_ge(s_eh, g * E + (e + 1))
                nc.scalar.activation(eh[e][:], hps[e % 2][:], ACT.Gelu).then_inc(s_eg, 1)

            def body(g, u):
                static = isinstance(g, int)
                ahead = not (static and g >= NG - 1)
                for e in range(E):
                    if ahead and 2 <= e < 2 + FB:
                        gates(g + 1, e - 2)
                    if not (static and g < 0):
                        expert(g, e)
                if ahead:
                    act.wait_ge(s_xps, g + 2)
                    nc.scalar.copy(xT[1 - u][:], xps[:, 0:GT])
                    nc.scalar.copy(x_hi[1 - u][:], xps[:, 0:GT]).then_inc(s_xhi, 1)
            steps(act, body)

        @block.vector
        def _(dve):
            dve.wait_ge(s_const, 2)

            def gated(k, c):
                dve.wait_ge(s_gate, k * FB + (c + 1))
                nc.vector.scalar_tensor_tensor(out=hid[:, c, :], in0=fps[c % 2][:, GT:2 * GT], scalar=b1[:, c:c + 1],
                                               in1=gate[:, c % 2, :], op0=ALU.add, op1=ALU.mult).then_inc(s_hid, 1)

            def sum_xy(k, u):
                dve.wait_ge(s_x[u], landed(k, u))
                dve.wait_ge(intake.s_yb, k + 1)
                nc.vector.tensor_tensor(x[u][:], x[u][:], y[:, bass.ds(k * 2, 2), :], ALU.add).then_inc(s_xy0, 1)

            def after_feed_forward(k, u):
                dve.wait_ge(s_ff, k + 1)
                dve.wait_ge(s_xy0, k + 1)
                nc.vector.tensor_tensor(x[u][:], fps[0][:, 0:2 * D].rearrange("p (t d) -> p t d", d=D), x[u][:],
                                        ALU.add).then_inc(s_xy, 1)
                dve.wait_ge(s_xy, k + 1)
                for t in range(2):
                    ins = nc.vector.bn_stats(xstats[:, t, :], x[u][:, t, :])
                ins.then_inc(s_xs, 1)
                dve.wait_ge(s_xs, 1)
                dve.wait_ge(s_xs, k + 1)
                for t in range(2):
                    ins = nc.vector.bn_aggr(xmv[:, t, :], xstats[:, t, :])
                ins.then_inc(s_xa, 1)
                dve.wait_ge(s_xa, k + 1)
                nc.vector.tensor_scalar(xvar[:], xmv[:, :, 1], EPS, None, ALU.add).then_inc(s_xv, 1)

            def normalised_x(k, u):
                dve.wait_ge(s_xr, k + 1)
                for t in range(2):
                    ins = nc.vector.tensor_scalar(xn[:, t, :], x[u][:, t, :], xmv[:, t, 0:1], xrstd[:, t:t + 1],
                                                  ALU.subtract, ALU.mult)
                ins.then_inc(s_xn, 1)

            def transposed_x(k, u):
                dve.wait_ge(s_xhi, k + 1)
                nc.vector.tensor_tensor(x_lo[u][:], xps[:, 0:GT], x_hi[u][:].bitcast(F32), ALU.subtract).then_inc(s_xT, 1)

            def route(k, u):
                dve.wait_ge(s_lg, k + 1)
                nc.vector.tensor_copy(logits[:], xps[:, GT:GT + 2 * E].rearrange("p (t e) -> p t e", e=E)).then_inc(s_lgs, 1)
                dve.wait_ge(s_lgs, 1)
                dve.wait_ge(s_lgs, k + 1)
                for t in range(2):
                    ins = nc.vector.max(best[:, t, :], logits[:, t, :])
                ins.then_inc(s_best, 1)
                dve.wait_ge(s_best, 1)
                dve.wait_ge(s_best, k + 1)
                for t in range(2):
                    nc.vector.max_index(place[:, t, :], best[:, t, :], logits[:, t, :])
                nc.vector.tensor_tensor(diff[:], best[:, :, 1], best[:, :, 0], ALU.subtract).then_inc(s_place, 1)

            def mixture(k, u):
                dve.wait_ge(s_place, k + 1)
                nc.vector.tensor_copy(placef[:], place[:, :, 0:2])
                dve.wait_ge(s_ratio, k + 1)
                nc.vector.tensor_scalar(denom[:], ratio[:], 1.0, None, ALU.add).then_inc(s_soft, 1)
                dve.wait_ge(s_soft, k * 4 + 1)
                nc.vector.reciprocal(p1[:], denom[:]).then_inc(s_soft, 1)
                dve.wait_ge(s_soft, k * 4 + 2)
                nc.vector.tensor_tensor(p2[:], p1[:], ratio[:], ALU.mult).then_inc(s_soft, 1)
                dve.wait_ge(s_soft, k * 4 + 3)
                for t in range(2):
                    ins = nc.vector.tensor_scalar(second[:, t, :], iota[:], placef[:, t, 1:2], p2[:, t:t + 1],
                                                  ALU.is_equal, ALU.mult)
                    ins = nc.vector.tensor_scalar(mix[u][:, t, :], iota[:], placef[:, t, 0:1], p1[:, t:t + 1],
                                                  ALU.is_equal, ALU.mult)
                ins.then_inc(s_soft, 1)
                dve.wait_ge(s_soft, k * 4 + 4)
                nc.vector.tensor_tensor(mix[u][:], mix[u][:], second[:], ALU.add).then_inc(s_mix, 1)

            def add_experts(g, u, job):
                half, t = job // 2, job % 2
                xt, ot = x[u][:, t, :], odd[:, t, :]
                dve.wait_ge(s_eo, g * 2 * HALVES + (job + 1))
                if job == 0:
                    dve.wait_ge(s_mix, g + 1)
                    if not (isinstance(g, int) and g == 0):
                        dve.wait_ge(s_acc, g * ADDS)
                for i in range(OB):
                    e = OB * half + i
                    if e >= 2:
                        before = job_start(2 * (half - 1) + t) + OB - 2 + i if i < 2 else job_start(job) + i - 2
                        dve.wait_ge(s_acc, g * ADDS + (before + 1))
                    src, w = ops[t][:, D * i:D * i + D], mix[u][:, t, e:e + 1]
                    if e == 1:
                        ins = nc.vector.tensor_scalar(ot, src, w, None, ALU.mult)
                    else:
                        to = ot if e % 2 else xt
                        ins = nc.vector.scalar_tensor_tensor(out=to, in0=src, scalar=w, in1=to, op0=ALU.mult, op1=ALU.add)
                    ins.then_inc(s_acc, 1)
                if half == HALVES - 1:
                    dve.wait_ge(s_acc, g * ADDS + (job_start(job) + OB))
                    nc.vector.tensor_tensor(xt, xt, ot, ALU.add).then_inc(s_acc, 1)

            def body(g, u):
                static = isinstance(g, int)
                now = not (static and g < 0)
                ahead = not (static and g >= NG - 1)
                stats_ahead = not (static and (g < 0 or g >= NG - 2))
                if ahead:
                    gated(g + 1, 0)
                if stats_ahead:
                    intake.statistics(dve, g + 2)
                if ahead:
                    for c in range(1, FB):
                        gated(g + 1, c)
                if now:
                    mixture(g, u)
                if ahead:
                    sum_xy(g + 1, 1 - u)
                if stats_ahead:
                    intake.normalised(dve, g + 2, u)
                if ahead:
                    after_feed_forward(g + 1, 1 - u)
                    normalised_x(g + 1, 1 - u)
                if now:
                    add_experts(g, u, 0)
                    add_experts(g, u, 1)
                if not (static and g >= NG - 2):
                    intake.modulate(dve, g + 2, u)
                if ahead:
                    transposed_x(g + 1, 1 - u)
                if now:
                    add_experts(g, u, 2)
                if ahead:
                    route(g + 1, 1 - u)
                if now:
                    add_experts(g, u, 3)
            steps(dve, body)

        @block.tensor
        def _(pe):
            def hidden(k, u, c):
                if c == 0:
                    pe.wait_ge(intake.s_h, k + 1)
                if isinstance(k, int) and k == 0 and c < 2:
                    pass
                elif c == 0:
                    pe.wait_ge(s_xy, k)
                else:
                    pe.wait_ge(s_hid, k * FB + (c - 1))
                for i, w in enumerate((FB + c, c)):
                    o = fps[c % 2][:, GT * i:GT * i + GT]
                    nc.tensor.matmul(o, w1_hi[:, P * w:P * w + P], h_hi[u][:], start=True, stop=False)
                    nc.tensor.matmul(o, w1_hi[:, P * w:P * w + P], h_lo[u][:], start=False, stop=False)
                    ins = nc.tensor.matmul(o, w1_lo[:, P * w:P * w + P], h_hi[u][:], start=False, stop=True)
                ins.then_inc(s_u, 1)

            def feed_forward_out(k):
                pe.wait_ge(s_hid, k * FB + FB)
                for t in range(2):
                    for c in range(FB):
                        ins = nc.tensor.matmul(fps[0][:, D * t:D * t + D], hid[:, c, P * t:P * t + P], w2[:, c, :],
                                               start=c == 0, stop=c == FB - 1)
                ins.then_inc(s_ff, 1)

            def transpose_x(k, u):
                pe.wait_ge(s_xn, k + 1)
                for t in range(2):
                    ins = nc.tensor.transpose(xps[:, P * t:P * t + P], xn[:, t, :], ident[:])
                ins.then_inc(s_xps, 1)

            def router_logits(k, u):
                pe.wait_ge(s_xT, k + 1)
                for t in range(2):
                    ins = nc.tensor.matmul(xps[:, GT + E * t:GT + E * t + E], xT[u][:, P * t:P * t + P], routerT,
                                           start=True, stop=True)
                ins.then_inc(s_lg, 1)

            def expert_hidden(g, u, e):
                if not (isinstance(g, int) and g == 0 and e < 2):
                    pe.wait_ge(s_eg, g * E + (e - 1))
                for c in range(EB):
                    o = hps[e % 2][:, GT * c:GT * c + GT]
                    nc.tensor.matmul(o, e1_hi[:, e, P * c:P * c + P], x_hi[u][:], start=True, stop=False)
                    nc.tensor.matmul(o, e1_hi[:, e, P * c:P * c + P], x_lo[u][:], start=False, stop=False)
                    ins = nc.tensor.matmul(o, e1_lo[:, e, P * c:P * c + P], x_hi[u][:], start=False, stop=True)
                ins.then_inc(s_eh, 1)

            def expert_out(g, job):
                half, t = job // 2, job % 2
                if half:
                    pe.wait_ge(s_acc, g * ADDS + (job_start(t) + OB))
                elif not (isinstance(g, int) and g == 0):
                    pe.wait_ge(s_acc, g * ADDS + (job_start(2 * HALVES - 2 + t) + OB - ADDS))
                for i in range(OB):
                    e = OB * half + i
                    if t == 0:
                        pe.wait_ge(s_eg, g * E + (e + 1))
                    for c in range(EB):
                        ins = nc.tensor.matmul(ops[t][:, D * i:D * i + D], eh[e][:, c, P * t:P * t + P], e2[:, e, c, :],
                                               start=c == 0, stop=c == EB - 1)
                ins.then_inc(s_eo, 1)

            def body(g, u):
                static = isinstance(g, int)
                now = not (static and g < 0)
                ahead = not (static and g >= NG - 1)
                for e in range(E - 1):
                    if ahead and 2 <= e < 2 + FB:
                        hidden(g + 1, 1 - u, e - 2)
                    if now:
                        expert_hidden(g, u, e)
                if ahead:
                    feed_forward_out(g + 1)
                if now:
                    expert_hidden(g, u, E - 1)
                    expert_out(g, 0)
                if not (static and g >= NG - 2):
                    intake.transpose_tokens(pe, g + 2, u)
                if now:
                    expert_out(g, 1)
                if ahead:
                    transpose_x(g + 1, 1 - u)
                if now:
                    expert_out(g, 2)
                    expert_out(g, 3)
                if ahead:
                    router_logits(g + 1, 1 - u)
            steps(pe, body)


def build(nc, inputs, out):
    BATCH, S, D = inputs["x"].shape
    INNER = inputs["attn1_wq"].shape[1]
    E, _, F = inputs["e_w1"].shape
    T = BATCH * S
    sizes = dict(S=S, D=D, BATCH=BATCH, H=INNER // 64, NG=T // (4 * S), E=E, F=F, DFF=inputs["ff_w2"].shape[0])
    inputs = dict(inputs)
    tiles = "(t two) s d -> t (two s) d"
    inputs["x"] = inputs["x"].rearrange(tiles, two=2)
    context = inputs["context"].rearrange(tiles, two=2)
    out = out.rearrange(tiles, two=2)
    H, NT, GT = sizes["H"], T // P, 4 * S

    with ExitStack() as ctx:
        def sb(n, shape, dt=F32):
            return ctx.enter_context(nc.sbuf_tensor(n, shape, dt))

        mem = dict(
            y=sb("y", [P, NT, D]),
            scale=sb("scale", [D, 3, BATCH]),
            shift=sb("shift", [D, 3, BATCH]),
            rowsT=sb("rowsT", [D, sizes["E"] + 2 * sizes["DFF"] // P]),
            bias=sb("bias", [P, 3 * D]),
            ident=sb("ident", [P, P]),
            neg_half=sb("neg_half", [P, NT]),
            z=[sb(f"z{u}", [P, 2, D]) for u in range(2)],
            hT=[sb(f"hT{u}", [D, GT]) for u in range(2)],
            c_in=[sb(f"c_in{u}", [P, 2, D]) for u in range(2)],
            sT=[sb(f"sT{u}", [D, GT]) for u in range(2)],
            s_hi=[sb(f"s_hi{u}", [D, GT], F32R) for u in range(2)],
            s_lo=[sb(f"s_lo{u}", [D, GT], F32R) for u in range(2)],
            w_hi=[sb(f"w_hi{u}", [D, 2, 2, S], F32R) for u in range(2)],
            w_lo=[sb(f"w_lo{u}", [D, 2, 2, S], F32R) for u in range(2)],
            stats=sb("stats", [P, 2, 6]),
            mv=sb("mv", [P, 2, 2]),
            var=sb("var", [P, 2]),
            rstd=sb("rstd", [P, 2]),
            tps=ctx.enter_context(nc.psum_tensor("tps", [P, BANK], F32)),
        )
        intake1 = Intake(nc, ctx, "in1", sizes, mem, 0, mem["bias"][:, 0:D], None)
        intake2 = Intake(nc, ctx, "in2", sizes, mem, 1, mem["bias"][:, D:2 * D], intake1, context)
        intake3 = Intake(nc, ctx, "in3", sizes, mem, 2, mem["bias"][:, 2 * D:3 * D], intake2, swaps=False)

        def products(stack, a):
            return [stack.enter_context(nc.sbuf_tensor(f"{n}{a}", shape, F32R))
                    for n, shape in (("A_hi", [D, H, D]), ("A_lo", [D, H, D]), ("B_hi", [D, 2, H // 2, D]),
                                     ("B_lo", [D, 2, H // 2, D]))]

        second = products(ctx, 1)
        with ExitStack() as inner:
            mem["attn"] = [products(inner, 0), second]
            setup_phase(nc, sizes, mem, inputs, intake1)
            attention_phase(nc, "attn1", sizes, mem, intake1, mem["attn"][0], intake2)

        E, F, DFF = sizes["E"], sizes["F"], sizes["DFF"]
        mem.update(
            w1=sb("w1", [D, 2 * DFF]), w1_hi=sb("w1_hi", [D, 2 * DFF], F32R), w1_lo=sb("w1_lo", [D, 2 * DFF], F32R),
            e1=sb("e1", [D, E * F]), e1_hi=sb("e1_hi", [D, E * F], F32R), e1_lo=sb("e1_lo", [D, E * F], F32R),
            w2=sb("w2", [P, DFF // P, D]), e2=sb("e2", [P, E, F // P, D]),
        )
        s_load = ctx.enter_context(nc.semaphore("ff_weights_loaded"))
        s_split = ctx.enter_context(nc.semaphore("ff_weights_split"))
        PIECE, STEPS = 512, (0, sizes["NG"] - 3, sizes["NG"] - 2, sizes["NG"] - 1)
        pieces = [(n, o) for n, width in (("w1", 2 * DFF), ("e1", E * F)) for o in range(0, width, PIECE)]
        each = -(-len(pieces) // len(STEPS))

        def load_weights(sp):
            sp.dma_start(mem["w1"][:], inputs["ff_w1"]).then_inc(s_load, 16)
            sp.dma_start(mem["e1"][:].rearrange("d (e f) -> d e f", e=E), inputs["e_w1"].rearrange("e d f -> d e f")).then_inc(s_load, 16)
            sp.dma_start(mem["w2"][:], inputs["ff_w2"].rearrange("(c p) d -> p c d", p=P)).then_inc(s_load, 16)
            sp.dma_start(mem["e2"][:], inputs["e_w2"].rearrange("e (c p) d -> p e c d", p=P)).then_inc(s_load, 16)

        def split_weights(pool, step):
            if step not in STEPS:
                return
            pool.wait_ge(s_load, 16 * 4)
            at = STEPS.index(step) * each
            for i, (n, o) in enumerate(pieces[at:at + each]):
                w, hi, lo = (mem[n + part][:, o:o + PIECE] for part in ("", "_hi", "_lo"))
                nc.gpsimd.tensor_copy(hi, w).then_inc(s_split, 1)
                pool.wait_ge(s_split, at + i + 1)
                nc.gpsimd.tensor_tensor(lo, w, hi.bitcast(F32), ALU.subtract)

        attention_phase(nc, "attn2", sizes, mem, intake2, second, intake3, (load_weights, split_weights))
        feed_forward_phase(nc, sizes, mem, intake3, inputs, out)


_INS = ["x", "cond_1024", "ctx_1024"] + [f"L0_xcond_{n}" for n in (
    "attn1_wq", "attn1_wk", "attn1_wv", "attn1_wo", "attn1_bo", "attn2_wq", "attn2_wk", "attn2_wv", "attn2_wo",
    "attn2_bo", "ff_w1", "ff_b1", "ff_w2", "ff_b2", "norm1_w", "norm1_b", "norm2_w", "norm2_b", "norm3_w",
    "norm3_b")] + ["L0_ffn_router_w", "L0_ffn_w1", "L0_ffn_w2"]
_NAMES = {"cond_1024": "cond", "ctx_1024": "context", "L0_ffn_router_w": "router_w", "L0_ffn_w1": "e_w1",
          "L0_ffn_w2": "e_w2"}


def kernel(**inputs):
    import numpy as _np
    import concourse.bacc as _bacc
    from concourse import mybir as _mybir
    from concourse.bass_utils import run_bass_kernel_spmd as _run

    nc = _bacc.Bacc("TRN2", target_bir_lowering=False, num_devices=1)
    arrays, aps = {}, {}
    for name in _INS:
        a = _np.ascontiguousarray(inputs[name])
        arrays[f"in_{name}"] = a
        short = _NAMES.get(name, name.replace("L0_xcond_", ""))
        aps[short] = nc.dram_tensor(f"in_{name}", a.shape, _mybir.dt.from_np(a.dtype), kind="ExternalInput").ap()
    out = nc.dram_tensor("out", inputs["x"].shape, F32, kind="ExternalOutput").ap()
    build(nc, aps, out)
    r = _run(nc, [arrays], core_ids=[0])
    return r.results[0]["out"]
```

```python
from contextlib import ExitStack

import concourse.bass as bass
from concourse import mybir

F32 = mybir.dt.float32
F32R = mybir.dt.float32r
U32 = mybir.dt.uint32
ALU = mybir.AluOpType
ACT = mybir.ActivationFunctionType
AX_X = mybir.AxisListType.X

P = 128
BANK = 512
RING = 4
EPS = 1e-5


def landed(k, u):
    return (k - u) * 8 + 16


class Intake:

    def __init__(self, nc, ctx, name, sizes, mem, norm, bias, before, context=None, swaps=True):
        def sem(n):
            return ctx.enter_context(nc.semaphore(f"{name}_{n}"))

        self.nc, self.mem, self.norm, self.bias, self.before, self.context = nc, mem, norm, bias, before, context
        self.swaps = swaps
        self.S, self.D, self.GT, self.NB, self.NG = sizes["S"], sizes["D"], 4 * sizes["S"], 4, sizes["NG"]
        self.z, self.hT = mem["z"], mem["hT"]
        self.sT = mem["sT"] if context is not None else mem["hT"]
        self.s_ctx = [sem(f"ctx_loaded{u}") for u in range(2)]
        self.s_stats0 = sem("stats0")
        self.s_stats = sem("stats")
        self.s_aggr = sem("aggr")
        self.s_var = sem("var")
        self.s_rstd = sem("rstd")
        self.s_z = sem("z")
        self.s_yb = sem("y_bias")
        self.s_tps = sem("tps")
        self.s_hf = sem("hf")
        self.s_hi = sem("hi")
        self.s_h = sem("h")
        self.s_swap = sem("swap")

    def load_context(self, sp, k, u):
        sp.dma_start(self.mem["c_in"][u][:],
                     self.context[bass.ds(k * 2, 2)].rearrange("t p d -> p t d")).then_inc(self.s_ctx[u], 16)

    def statistics(self, dve, k):
        nc, y, stats, mv = self.nc, self.mem["y"], self.mem["stats"], self.mem["mv"]
        for t in range(2):
            ins = nc.vector.bn_stats(stats[:, t, :], y[:, bass.ds(k * 2 + t, 1), :])
        if isinstance(k, int) and k == 0:
            ins.then_inc(self.s_stats0, 1)
            dve.wait_ge(self.s_stats0, 1)
        else:
            ins.then_inc(self.s_stats, 1)
            dve.wait_ge(self.s_stats, 1)
            dve.wait_ge(self.s_stats, k)
        for t in range(2):
            ins = nc.vector.bn_aggr(mv[:, t, :], stats[:, t, :])
        ins.then_inc(self.s_aggr, 1)
        dve.wait_ge(self.s_aggr, k + 1)
        nc.vector.tensor_scalar(self.mem["var"][:], mv[:, :, 1], EPS, None, ALU.add).then_inc(self.s_var, 1)

    def rstd(self, pool, k):
        pool.wait_ge(self.s_var, k + 1)
        self.nc.gpsimd.tensor_tensor(self.mem["rstd"][:], self.mem["var"][:], self.mem["neg_half"][:, 0:2],
                                     ALU.pow).then_inc(self.s_rstd, 1)

    def normalised(self, dve, k, u):
        nc, y, mv = self.nc, self.mem["y"], self.mem["mv"]
        dve.wait_ge(self.s_rstd, k + 1)
        for t in range(2):
            ins = nc.vector.tensor_scalar(self.z[u][:, t:t + 1, :], y[:, bass.ds(k * 2 + t, 1), :], mv[:, t, 0:1],
                                          self.mem["rstd"][:, t:t + 1], ALU.subtract, ALU.mult)
        ins.then_inc(self.s_z, 1)
        dve.wait_ge(self.s_z, k + 1)
        yk = y[:, bass.ds(k * 2, 2), :]
        nc.vector.tensor_tensor(yk, yk, self.bias.unsqueeze(1).to_broadcast([P, 2, self.D]), ALU.add).then_inc(self.s_yb, 1)

    def transpose_tokens(self, pe, k, u):
        nc, tps, ident, GT = self.nc, self.mem["tps"], self.mem["ident"], self.GT
        pe.wait_ge(self.s_z, k + 1)
        if self.context is not None:
            pe.wait_ge(self.s_ctx[u], landed(k, u))
        if not (isinstance(k, int) and k == 0):
            pe.wait_ge(self.s_hf, k)
        elif self.before is not None:
            pe.wait_ge(self.before.s_hf, self.NG)
        for t in range(2):
            ins = nc.tensor.transpose(tps[:, P * t:P * t + P], self.z[u][:, t, :], ident[:])
        if self.context is not None:
            for t in range(2):
                ins = nc.tensor.transpose(tps[:, GT + P * t:GT + P * t + P], self.mem["c_in"][u][:, t, :], ident[:])
        ins.then_inc(self.s_tps, 1)

    def modulate(self, dve, k, u):
        nc, tps, S, NB, hT, sT = self.nc, self.mem["tps"], self.S, self.NB, self.hT[u], self.sT[u]
        s_hi, s_lo = self.mem["s_hi"][u], self.mem["s_lo"][u]
        dve.wait_ge(self.s_tps, k + 1)
        if self.context is not None:
            nc.vector.tensor_copy(sT[:], tps[:, self.GT:2 * self.GT])
        for b in range(NB):
            ins = nc.vector.tensor_scalar(hT[:, S * b:S * b + S], tps[:, S * b:S * b + S],
                                          self.mem["scale"][:, self.norm, bass.ds(k * NB + b, 1)],
                                          self.mem["shift"][:, self.norm, bass.ds(k * NB + b, 1)], ALU.mult, ALU.add)
        ins.then_inc(self.s_hf, 1)
        dve.wait_ge(self.s_hf, k + 1)
        nc.vector.tensor_copy(s_hi[:], sT[:]).then_inc(self.s_hi, 1)
        dve.wait_ge(self.s_hi, k + 1)
        nc.vector.tensor_tensor(s_lo[:], sT[:], s_hi[:].bitcast(F32), ALU.subtract).then_inc(self.s_h, 1)

    def swap(self, pool, k, u):
        nc, w_hi, w_lo = self.nc, self.mem["w_hi"][u], self.mem["w_lo"][u]
        pool.wait_ge(self.s_h, k + 1)
        whole, high = (a.rearrange("d (p b k) -> d p b k", p=2, b=2)
                       for a in (self.sT[u][:], self.mem["s_hi"][u][:].bitcast(F32)))
        for b in range(2):
            nc.gpsimd.tensor_tensor(w_lo[:, :, b, :], whole[:, :, 1 - b, :], high[:, :, 1 - b, :], ALU.subtract)
        for b in range(2):
            ins = nc.gpsimd.tensor_copy(w_hi[:, :, b, :], high[:, :, 1 - b, :])
        ins.then_inc(self.s_swap, 1)


class FeedForward:

    PIECE = 512

    def __init__(self, nc, ctx, sizes, mem, inputs, intake):
        def sb(n, shape, dt=F32):
            return ctx.enter_context(nc.sbuf_tensor(n, shape, dt))

        def sem(n):
            return ctx.enter_context(nc.semaphore(f"ff_{n}"))

        D, E, F, DFF, NG = sizes["D"], sizes["E"], sizes["F"], sizes["DFF"], sizes["NG"]
        self.nc, self.mem, self.inputs, self.intake = nc, mem, inputs, intake
        self.D, self.E, self.GT, self.FB = D, E, 4 * sizes["S"], DFF // P
        A_hi, A_lo, B_hi, _ = (a[:] for a in mem["attn"][0])
        w1_parts = B_hi.rearrange("d two h e -> d two (h e)")
        self.w1_hi, self.w1_lo = w1_parts[:, 0, :], w1_parts[:, 1, :]
        self.e1_hi, self.e1_lo = (a.rearrange("d h e -> d (h e)") for a in (A_hi, A_lo))
        self.w1, self.e1 = sb("w1", [D, 2 * DFF])[:], sb("e1", [D, E * F])[:]
        self.w2, self.e2 = sb("w2", [P, self.FB, D]), sb("e2", [P, E, F // P, D])
        self.b1 = mem["rowsT"][:, E:]
        self.gate = sb("gate", [P, 2, self.GT])
        self.hid = sb("hid", [P, self.FB, self.GT])
        self.x = [sb(f"x{u}", [P, 2, D]) for u in range(2)]
        self.banks = [mem["two_banks"][:, BANK * i:BANK * i + BANK] for i in range(2)]
        self.split_steps = (0, NG - 3, NG - 2, NG - 1)
        self.pieces = [(w, hi, lo, slice(o, o + self.PIECE))
                       for w, hi, lo in ((self.w1, self.w1_hi, self.w1_lo), (self.e1, self.e1_hi, self.e1_lo))
                       for o in range(0, w.shape[1], self.PIECE)]

        self.s_load = sem("weights_loaded")
        self.s_x = [sem(f"x_loaded{u}") for u in range(2)]
        self.s_split = sem("weights_split")
        self.s_u = sem("u")
        self.s_gate = sem("gate")
        self.s_hid = sem("hid")
        self.s_ff = sem("ff")
        self.s_xy = sem("xy")

    def load_weights(self, sp):
        e1 = self.e1.rearrange("d (e f) -> d e f", e=self.E)
        sp.dma_start(self.w1, self.inputs["ff_w1"]).then_inc(self.s_load, 16)
        sp.dma_start(e1, self.inputs["e_w1"].rearrange("e d f -> d e f")).then_inc(self.s_load, 16)
        sp.dma_start(self.w2[:], self.inputs["ff_w2"].rearrange("(c p) d -> p c d", p=P)).then_inc(self.s_load, 16)
        sp.dma_start(self.e2[:], self.inputs["e_w2"].rearrange("e (c p) d -> p e c d", p=P)).then_inc(self.s_load, 16)

    def load_x(self, sp, k, u):
        sp.dma_start(self.x[u][:], self.inputs["x"][bass.ds(k * 2, 2)].rearrange("t p d -> p t d")).then_inc(self.s_x[u], 16)

    def split_weights(self, pool, step):
        if step not in self.split_steps:
            return
        pool.wait_ge(self.s_load, 16 * 4)
        each = -(-len(self.pieces) // len(self.split_steps))
        at = self.split_steps.index(step) * each
        for i, (w, hi, lo, cols) in enumerate(self.pieces[at:at + each]):
            self.nc.gpsimd.tensor_copy(hi[:, cols], w[:, cols]).then_inc(self.s_split, 1)
            pool.wait_ge(self.s_split, 2 * (at + i) + 1)
            self.nc.gpsimd.tensor_tensor(lo[:, cols], w[:, cols], hi[:, cols].bitcast(F32), ALU.subtract).then_inc(self.s_split, 1)

    def hidden(self, pe, k, u, c):
        FB, GT, h_hi, h_lo = self.FB, self.GT, self.mem["s_hi"][u], self.mem["s_lo"][u]
        first = isinstance(k, int) and k == 0
        if c == 0:
            pe.wait_ge(self.intake.s_h, k + 1)
        if c == 0 and first:
            pe.wait_ge(self.s_split, 2 * len(self.pieces))
        elif c == 0:
            pe.wait_ge(self.s_xy, k)
        elif not (first and c == 1):
            pe.wait_ge(self.s_hid, k * FB + (c - 1))
        for i, w in enumerate((FB + c, c)):
            o, cols = self.banks[c % 2][:, GT * i:GT * i + GT], slice(P * w, P * w + P)
            self.nc.tensor.matmul(o, self.w1_hi[:, cols], h_hi[:], start=True, stop=False)
            self.nc.tensor.matmul(o, self.w1_hi[:, cols], h_lo[:], start=False, stop=False)
            ins = self.nc.tensor.matmul(o, self.w1_lo[:, cols], h_hi[:], start=False, stop=True)
        ins.then_inc(self.s_u, 1)

    def gates(self, act, k, c):
        FB = self.FB
        act.wait_ge(self.s_u, k * FB + (c + 1))
        if not (isinstance(k, int) and k == 0 and c < 2):
            act.wait_ge(self.s_hid, k * FB + (c - 1))
        self.nc.scalar.activation(self.gate[:, c % 2, :], self.banks[c % 2][:, 0:self.GT], ACT.Gelu,
                                  bias=self.b1[:, FB + c:FB + c + 1]).then_inc(self.s_gate, 1)

    def gated(self, dve, k, c):
        dve.wait_ge(self.s_gate, k * self.FB + (c + 1))
        self.nc.vector.scalar_tensor_tensor(out=self.hid[:, c, :], in0=self.banks[c % 2][:, self.GT:2 * self.GT],
                                            scalar=self.b1[:, c:c + 1], in1=self.gate[:, c % 2, :],
                                            op0=ALU.add, op1=ALU.mult).then_inc(self.s_hid, 1)

    def output(self, pe, k):
        pe.wait_ge(self.s_hid, k * self.FB + self.FB)
        D = self.D
        for t in range(2):
            for c in range(self.FB):
                ins = self.nc.tensor.matmul(self.banks[0][:, D * t:D * t + D], self.hid[:, c, P * t:P * t + P],
                                            self.w2[:, c, :], start=c == 0, stop=c == self.FB - 1)
        ins.then_inc(self.s_ff, 1)


def attention_phase(nc, sizes, mem, intakes, weights, ff):
    S, D, H, NG = sizes["S"], sizes["D"], sizes["H"], sizes["NG"]
    GT, NB, NP = 4 * S, 4, 2
    HC = BANK // S
    QC = BANK // D
    ATTENTIONS = len(weights)
    y, ident, hT, s_hi_buf, s_lo_buf = mem["y"], mem["ident"], mem["hT"], mem["s_hi"], mem["s_lo"]
    G_JOBS, T_JOBS, V_JOBS = H * GT // BANK, H // 2 // QC, 2 * (H // 2) // QC
    JOBS = G_JOBS + 2 * T_JOBS + 2 * V_JOBS

    with ExitStack() as ctx:
        def sb(n, shape, dt=F32):
            return ctx.enter_context(nc.sbuf_tensor(f"attn_{n}", shape, dt))

        def ps(n, shape):
            return ctx.enter_context(nc.psum_tensor(f"attn_{n}", shape, F32))

        def sem(n):
            return ctx.enter_context(nc.semaphore(f"attn_{n}"))

        G = sb("G", [D, H // 2, 4, NP, S])
        V = [sb(f"V{u}", [P, NB, H // 2, D]) for u in range(2)]
        Pr = [[sb(f"P{u}{p}", [P, H, S]) for p in range(NP)] for u in range(2)]
        PT = sb("PT", [P, NP, H // 2, P])
        top = sb("top", [P, H])
        total = sb("total", [P, H])
        inv = [sb(f"inv{p}", [P, H]) for p in range(NP)]

        ring = [ps(f"ring{i}", [P, BANK]) for i in range(RING)]
        Sps = mem["two_banks"]
        ops = ps("ops", [P, BANK])

        s_full = sem("ring_full")
        s_free = sem("ring_free")
        s_S = sem("scores")
        s_top = sem("top")
        s_sub = sem("sub")
        s_exp = sem("exp")
        s_sum = sem("sum")
        s_inv = sem("inv")
        s_P = sem("P")
        s_o = sem("o")
        s_y = sem("y")

        block = ctx.enter_context(nc.Block())

        def turn(n, local):
            return local if isinstance(n, int) and n == 0 else n * JOBS + (local - 2 * T_JOBS)

        def locals_of(n):
            if isinstance(n, int) and n == 0:
                return [G_JOBS, G_JOBS + V_JOBS], None
            if isinstance(n, int) and n == ATTENTIONS * NG:
                return None, [0, T_JOBS]
            t0 = G_JOBS
            return [t0 + T_JOBS, t0 + 2 * T_JOBS + V_JOBS], [t0, t0 + T_JOBS + V_JOBS]

        def steps(eng, body):
            for a in range(ATTENTIONS):
                body(a, 0, 0)
                with eng.Fori(0, NG - 5, 2) as i:
                    body(a, i + 1, 1)
                    body(a, i + 2, 0)
                for g in range(NG - 3, NG):
                    body(a, g, g % 2)
            body(ATTENTIONS - 1, NG, 0)

        ff_blocks = (range(0, 1), range(1, ff.FB))

        def intake_of(a, g):
            return (intakes[a + 1], g - NG) if isinstance(g, int) and g >= NG else (intakes[a], g)

        @block.sync
        def _(sp):
            intake = intakes[1]
            intake.load_context(sp, 0, 0)
            intake.load_context(sp, 1, 1)
            ff.load_weights(sp)
            ff.load_x(sp, 0, 0)
            ff.load_x(sp, 1, 1)

            def later(k, u):
                sp.wait_ge(intake.s_tps, k - 1)
                intake.load_context(sp, k, u)
            with sp.Fori(0, NG - 3, 2) as i:
                later(i + 2, 0)
                later(i + 3, 1)

        @block.gpsimd
        def _(pool):
            def normalise(n, u, p):
                pool.wait_ge(s_inv, n * 2 + (p + 1))
                pr = Pr[u][p]
                nc.gpsimd.tensor_tensor(pr[:], pr[:], inv[p][:].unsqueeze(2).to_broadcast([P, H, S]),
                                        ALU.mult).then_inc(s_P, 1)

            def body(a, g, u):
                n = g + a * NG
                static = isinstance(g, int)
                if static and g == NG:
                    return
                intake, k = intake_of(a, g + 2)
                intake.rstd(pool, k)
                normalise(n, u, 0)
                intake, k = intake_of(a, g + 1)
                if intake.swaps:
                    intake.swap(pool, k, 1 - u)
                normalise(n, u, 1)
                if static and a == 1:
                    ff.split_weights(pool, g)
            steps(pool, body)

        @block.scalar
        def _(act):
            def copy_out(step, local, out):
                act.wait_ge(s_full, turn(step, local) + 1)
                nc.scalar.copy(out, ring[local % RING][:]).then_inc(s_free, 1)

            def exps(n, u, p):
                act.wait_ge(s_sub, n * 2 + (p + 1))
                nc.scalar.activation(Pr[u][p][:], Pr[u][p][:], ACT.Exp).then_inc(s_exp, 1)

            def body(a, g, u):
                n = g + a * NG
                last = isinstance(g, int) and g == NG
                values, transposed = locals_of(n)
                if not last:
                    for j in range(G_JOBS):
                        copy_out(n, j, G[:, j, :, :, :])
                for p in range(NP):
                    if transposed:
                        for c in range(T_JOBS):
                            copy_out(n, transposed[p] + c, PT[:, p, QC * c:QC * c + QC, :])
                    if last:
                        for c in ff_blocks[p]:
                            ff.gates(act, 0, c)
                    if not last:
                        for i in range(V_JOBS):
                            if i == V_JOBS - 1:
                                exps(n, u, p)
                            c, par = i // 2, i % 2
                            act.wait_ge(s_full, turn(n, values[p] + i) + 1)
                            for half in range(2):
                                rows, b = slice(S * half, S * half + S), half ^ par
                                ins = nc.scalar.copy(V[u][rows, 2 * p + b, QC * c:QC * c + QC, :],
                                                     ring[(values[p] + i) % RING][rows, :])
                            ins.then_inc(s_free, 1)
            steps(act, body)

        @block.vector
        def _(dve):
            def subtract_max(n, u, p):
                dve.wait_ge(s_S, n * 2 + (p + 1))
                sc = Sps[:].rearrange("q (h k) -> q h k", k=S)
                nc.vector.tensor_reduce(top[:], sc, AX_X, ALU.max).then_inc(s_top, 1)
                dve.wait_ge(s_top, n * 2 + (p + 1))
                nc.vector.tensor_tensor(Pr[u][p][:], sc, top[:].unsqueeze(2).to_broadcast([P, H, S]),
                                        ALU.subtract).then_inc(s_sub, 1)

            def sums(n, u, p):
                dve.wait_ge(s_exp, n * 2 + (p + 1))
                nc.vector.tensor_reduce(total[:], Pr[u][p][:], AX_X, ALU.add).then_inc(s_sum, 1)
                dve.wait_ge(s_sum, n * 2 + (p + 1))
                nc.vector.reciprocal(inv[p][:], total[:]).then_inc(s_inv, 1)

            def residual(a, g, p):
                dve.wait_ge(s_o, g * 2 + (2 * NG * a + p + 1))
                if p == 0:
                    dve.wait_ge(intakes[a].s_yb, g + 1)
                yt = y[:, bass.ds(g * 2 + p, 1), :]
                nc.vector.tensor_tensor(yt, ops[:, 0:D].unsqueeze(1), yt, ALU.add).then_inc(s_y, 1)

            def body(a, g, u):
                n = g + a * NG
                static = isinstance(g, int)
                now = not (static and g == NG)
                first = static and n == 0
                before = (a, g - 1) if not (static and g == 0) else (a - 1, NG - 1)
                if now:
                    intake2, k2 = intake_of(a, g + 2)
                    intake1, k1 = intake_of(a, g + 1)
                    if intake2 is not intakes[a]:
                        dve.wait_ge(s_y, 2 * NG * a + 2 * k2 + 2)
                    intake2.statistics(dve, k2)
                    subtract_max(n, u, 0)
                if not now:
                    ff.gated(dve, 0, 0)
                if not first:
                    residual(*before, 0)
                if now:
                    sums(n, u, 0)
                    if first:
                        intake1.modulate(dve, k1, 1 - u)
                    subtract_max(n, u, 1)
                    if not first:
                        intake1.modulate(dve, k1, 1 - u)
                    intake2.normalised(dve, k2, u)
                    sums(n, u, 1)
                else:
                    for c in ff_blocks[1][:-1]:
                        ff.gated(dve, 0, c)
                if not first:
                    residual(*before, 1)
                if not now:
                    ff.gated(dve, 0, ff.FB - 1)
            steps(dve, body)

        @block.tensor
        def _(pe):
            def turned(step, local):
                n = turn(step, local)
                if not (isinstance(n, int) and n < RING):
                    pe.wait_ge(s_free, n - (RING - 1))
                return ring[local % RING]

            def keys(a, g, u):
                A_hi, A_lo, _, _ = weights[a]
                pe.wait_ge(intakes[a].s_h, g + 1)
                for j in range(G_JOBS):
                    bank = turned(g + a * NG, j)
                    places = bank[:].rearrange("d (q p k) -> d p q k", p=NP, k=S)
                    for i in range(2):
                        out, h = places[:, :, slice(0, 4, 3) if i == 0 else slice(1, 3), :], 2 * j + i
                        nc.tensor.matmul(out, A_hi[:, h, :], s_hi_buf[u][:], start=True, stop=False)
                        nc.tensor.matmul(out, A_hi[:, h, :], s_lo_buf[u][:], start=False, stop=False)
                        ins = nc.tensor.matmul(out, A_lo[:, h, :], s_hi_buf[u][:], start=False, stop=True)
                    ins.then_inc(s_full, 1)

            def scores(n, u, p):
                pe.wait_ge(s_free, turn(n, G_JOBS))
                if not (isinstance(n, int) and n == 0 and p == 0):
                    pe.wait_ge(s_sub, n * 2 + p)
                for c in range(H // HC):
                    bank = Sps[:, BANK * c:BANK * c + BANK]
                    for b in range(2):
                        tok = S * (2 * p + b)
                        ins = nc.tensor.matmul(bank[S * b:S * b + S, :], hT[u][:, tok:tok + S],
                                               G[:, HC // 2 * c:HC // 2 * c + HC // 2, 2 * b:2 * b + 2, p, :],
                                               start=True, stop=True)
                ins.then_inc(s_S, 1)

            def values(a, g, u, p, local):
                _, _, B_hi, B_lo = weights[a]
                if p == 0:
                    pe.wait_ge(intakes[a].s_swap, g + 1)
                for i in range(V_JOBS):
                    c, par = i // 2, i % 2
                    bank = turned(g + a * NG, local + i)
                    if par:
                        hi, lo = (w[u][:, p, :, :].rearrange("d b k -> d (b k)") for w in (mem["w_hi"], mem["w_lo"]))
                    else:
                        hi, lo = (w[u][:, P * p:P * p + P] for w in (s_hi_buf, s_lo_buf))
                    cols = slice(QC * c, QC * c + QC)
                    nc.tensor.matmul(bank[:], hi, B_hi[:, par, cols, :], start=True, stop=False)
                    nc.tensor.matmul(bank[:], lo, B_hi[:, par, cols, :], start=False, stop=False)
                    ins = nc.tensor.matmul(bank[:], hi, B_lo[:, par, cols, :], start=False, stop=True)
                    ins.then_inc(s_full, 1)

            def transpose_probabilities(step, u, p, local):
                pe.wait_ge(s_P, step * 2 + (p - 1))
                pr = Pr[u][p][:].rearrange("q h k -> q (h k)")
                for c in range(T_JOBS):
                    bank = turned(step, local + c)
                    for i in range(QC):
                        n = QC * c + i
                        ins = nc.tensor.transpose(bank[:, P * i:P * i + P], pr[:, P * n:P * n + P], ident[:])
                    ins.then_inc(s_full, 1)

            def weighted_sum(step, u, p, local):
                pe.wait_ge(s_free, turn(step, local + T_JOBS))
                if not (isinstance(step, int) and step == 1 and p == 0):
                    pe.wait_ge(s_y, step * 2 + (p - 2))
                for n in range(H // 2):
                    for b in range(2):
                        ins = nc.tensor.matmul(ops[S * b:S * b + S, 0:D], PT[:, p, n, S * b:S * b + S],
                                               V[u][:, 2 * p + b, n, :], start=n == 0, stop=n == H // 2 - 1)
                ins.then_inc(s_o, 1)

            def body(a, g, u):
                n = g + a * NG
                now = not (isinstance(g, int) and g == NG)
                vl, tl = locals_of(n)
                if now:
                    intake, k = intake_of(a, g + 1)
                    keys(a, g, u)
                if tl:
                    transpose_probabilities(n, 1 - u, 0, tl[0])
                if not now:
                    pe.wait_ge(s_sub, 2 * ATTENTIONS * NG)
                    ff.hidden(pe, 0, 0, 0)
                if now:
                    scores(n, u, 0)
                    values(a, g, u, 0, vl[0])
                if tl:
                    weighted_sum(n, 1 - u, 0, tl[0])
                    transpose_probabilities(n, 1 - u, 1, tl[1])
                else:
                    intake.transpose_tokens(pe, k, 1 - u)
                if now:
                    scores(n, u, 1)
                    if tl:
                        intake.transpose_tokens(pe, k, 1 - u)
                    values(a, g, u, 1, vl[1])
                else:
                    for c in ff_blocks[1][:-1]:
                        ff.hidden(pe, 0, 0, c)
                if tl:
                    weighted_sum(n, 1 - u, 1, tl[1])
                if not now:
                    ff.hidden(pe, 0, 0, ff.FB - 1)
                    ff.output(pe, 0)
            steps(pe, body)


def setup_phase(nc, sizes, mem, inputs, following):
    S, D, H, NG, BATCH = sizes["S"], sizes["D"], sizes["H"], sizes["NG"], sizes["BATCH"]
    HP = H // 2
    NT = 2 * NG
    XC = 4
    dh = S
    y, scale, shift, ident = mem["y"], mem["scale"], mem["shift"], mem["ident"]

    with ExitStack() as ctx:
        def sb(n, shape, dt=F32):
            return ctx.enter_context(nc.sbuf_tensor(f"set_{n}", shape, dt))

        def sem(n):
            return ctx.enter_context(nc.semaphore(f"set_{n}"))

        x = sb("x", [P, NT, D])
        E = sizes["E"]
        NROW = BATCH + 6 + E + 2 * sizes["DFF"] // P
        rows = sb("rows", [NROW, D])
        rowsT = sb("rowsT", [D, BATCH + 6])
        nw = sb("nw", [D, 3, 2 * D])
        biases = sb("biases", [1, 3, D])
        ones = sb("ones", [1, P])
        w_in = [[sb(f"w{m}{a}", [D, H * dh]) for m in range(3)] for a in range(2)]
        wo = [sb(f"wo{a}", [P, HP, D]) for a in range(2)]
        wT = [sb(f"wT{m}", [P, HP, D]) for m in range(3)]
        stats = sb("stats", [P, NT, 6])
        mv = sb("mv", [P, NT, 2])
        var = sb("var", [P, NT])
        rstd = sb("rstd", [P, NT])
        ring = [ctx.enter_context(nc.psum_tensor(f"set_ring{i}", [P, BANK], F32)) for i in range(5)]
        misc = [mem["two_banks"][:, BANK * i:BANK * i + BANK] for i in range(2)]
        NR = len(ring)

        s_x = [sem(f"x{i}") for i in range(XC)]
        s_cond0 = sem("cond_loaded")
        s_cond = sem("small_loaded")
        s_w = [[sem(f"w{m}{a}_loaded") for m in range(4)] for a in range(2)]
        s_ident = sem("ident")
        s_ones = sem("ones")
        s_half = sem("half")
        s_rowsT = sem("rowsT")
        s_cT = sem("cT")
        s_emb = sem("emb")
        s_bias = sem("bias")
        s_stats = sem("stats")
        s_aggr = sem("aggr")
        s_var = sem("var")
        s_rstd = sem("rstd")
        s_full = sem("full")
        s_free = sem("free")
        s_lo = sem("lo")
        s_y = sem("y")
        s_mod = sem("mod")
        block = ctx.enter_context(nc.Block())

        TB = HP * P // BANK
        AB = H * D // BANK
        PB = BANK // P
        TURNS = 3 * TB + 2 * AB
        FACTOR = (dh ** -0.5, 1.0)
        per = NT // XC

        def heads_of(a, product, low, i):
            par, c = i // (AB // 2), i % (AB // 2)
            w = mem["attn"][a][2 * product + low]
            if product:
                return w[:, par, PB * c:PB * c + PB, :]
            return w[:].rearrange("p (n two) d -> p n two d", two=2)[:, PB * c:PB * c + PB, par, :]

        def products_before(n):
            return sum(min(max(n - a * TURNS - 3 * TB, 0), 2 * AB) for a in range(2))

        @block.sync
        def _(sp):
            for a in range(2):
                for m, n in enumerate(("wq", "wk", "wv")):
                    sp.dma_start(w_in[a][m][:], inputs[f"attn{a + 1}_{n}"]).then_inc(s_w[a][m], 16)
                sp.dma_start(wo[a][:], inputs[f"attn{a + 1}_wo"].rearrange("(h p) d -> p h d", p=P)).then_inc(s_w[a][3], 16)

        @block.gpsimd
        def _(pool):
            nc.gpsimd.memset(ident[:], 0.0).then_inc(s_ident, 1)
            pool.wait_ge(s_ident, 1)
            nc.gpsimd.affine_select(out=ident[:], in_=ident[:], compare_op=ALU.not_equal, fill=1.0, base=0,
                                    pattern=[[-1, P]], channel_multiplier=1).then_inc(s_ident, 1)
            for i in range(3):
                pool.dma_start(nw[:, i, :], inputs[f"norm{i + 1}_w"]).then_inc(s_cond, 16)
                pool.dma_start(rows[BATCH + 2 * i:BATCH + 2 * i + 2, :],
                               inputs[f"norm{i + 1}_b"].rearrange("(c p) -> c p", p=D)).then_inc(s_cond, 16)
            for i, n in enumerate(("attn1_bo", "attn2_bo", "ff_b2")):
                pool.dma_start(biases[:, i, :], inputs[n].rearrange("(a n) -> a n", a=1)).then_inc(s_cond, 16)
            pool.dma_start(rows[BATCH + 6:BATCH + 6 + E, :], inputs["router_w"]).then_inc(s_cond, 16)
            pool.dma_start(rows[BATCH + 6 + E:, :], inputs["ff_b1"].rearrange("(c p) -> c p", p=P)).then_inc(s_cond, 16)
            nc.gpsimd.memset(ones[:], 1.0).then_inc(s_ones, 1)
            nc.gpsimd.memset(mem["neg_half"][:], -0.5).then_inc(s_half, 1)
            pool.wait_ge(s_half, 1)
            for i in range(XC):
                piece = slice(i * per, i * per + per)
                pool.wait_ge(s_var, i + 1)
                nc.gpsimd.tensor_tensor(rstd[:, piece], var[:, piece], mem["neg_half"][:, piece], ALU.pow).then_inc(s_rstd, 1)
            following.rstd(pool, 0)

            def normalised(first, end):
                pool.wait_ge(s_rstd, XC)
                for t in range(first, end):
                    nc.gpsimd.tensor_scalar(y[:, t, :], x[:, t, :], mv[:, t, 0:1], rstd[:, t:t + 1],
                                            ALU.subtract, ALU.mult)
            normalised(NT - per, NT - per // 2)
            following.rstd(pool, 1)
            normalised(NT - per // 2, NT)
            following.swap(pool, 0, 0)

        @block.scalar
        def _(act):
            act.dma_start(rows[0:BATCH, :], inputs["cond"]).then_inc(s_cond0, 16)
            for i in range(XC):
                act.dma_start(x[:, i * per:i * per + per, :],
                              inputs["x"][i * per:i * per + per].rearrange("t p d -> p t d")).then_inc(s_x[i], 16)
            for a in range(2):
                n = a * TURNS
                for m in range(3):
                    for c in range(TB):
                        act.wait_ge(s_full, n + 1)
                        nc.scalar.copy(wT[m][:, PB * c:PB * c + PB, :], ring[n % NR][:]).then_inc(s_free, 1)
                        n += 1
                for product in range(2):
                    for i in range(AB):
                        act.wait_ge(s_full, n + 1)
                        nc.scalar.activation(heads_of(a, product, 0, i), ring[n % NR][:].rearrange("p (n d) -> p n d", d=D),
                                             ACT.Copy, scale=FACTOR[product]).then_inc(s_free, 1)
                        n += 1

        @block.vector
        def _(dve):
            def statistics(i):
                piece = slice(i * per, i * per + per)
                dve.wait_ge(s_x[i], 16)
                for t in range(i * per, i * per + per):
                    nc.vector.bn_stats(stats[:, t, :], x[:, t, :]).then_inc(s_stats, 1)
                dve.wait_ge(s_stats, i * per + per)
                for t in range(i * per, i * per + per):
                    nc.vector.bn_aggr(mv[:, t, :], stats[:, t, :]).then_inc(s_aggr, 1)
                dve.wait_ge(s_aggr, i * per + per)
                nc.vector.tensor_scalar(var[:, piece], mv[:, piece, 1], EPS, None, ALU.add).then_inc(s_var, 1)

            def normalised(first, end):
                dve.wait_ge(s_rstd, (end - 1) // per + 1)
                for t in range(first, end):
                    nc.vector.tensor_scalar(y[:, t, :], x[:, t, :], mv[:, t, 0:1], rstd[:, t:t + 1],
                                            ALU.subtract, ALU.mult).then_inc(s_y, 1)

            def low_parts(a, product, tiles=0):
                for i in range(AB):
                    n = a * TURNS + 3 * TB + product * AB + i
                    dve.wait_ge(s_free, n + 1)
                    nc.vector.scalar_tensor_tensor(out=heads_of(a, product, 1, i),
                                                   in0=ring[n % NR][:].rearrange("p (n d) -> p n d", d=D),
                                                   scalar=FACTOR[product], in1=heads_of(a, product, 0, i).bitcast(F32),
                                                   op0=ALU.mult, op1=ALU.subtract).then_inc(s_lo, 1)
                    if tiles:
                        normalised(tiles // AB * i, tiles // AB * (i + 1))

            statistics(0)
            statistics(1)
            low_parts(0, 0, 2 * per)
            statistics(2)
            low_parts(0, 1)
            dve.wait_ge(s_rowsT, 1)
            nc.vector.tensor_copy(mem["rowsT"][:], misc[0][:, BATCH + 6:NROW])
            nc.vector.tensor_copy(rowsT[:], misc[0][:, 0:BATCH + 6]).then_inc(s_cT, 1)
            dve.wait_ge(s_y, per)
            following.statistics(dve, 0)
            statistics(3)
            normalised(2 * per, 3 * per)
            dve.wait_ge(s_emb, 1)
            for i in range(3):
                nb = rowsT[:, BATCH + 2 * i:BATCH + 2 * i + 2]
                src = misc[1][:, 2 * BATCH * i:2 * BATCH * i + 2 * BATCH]
                nc.vector.tensor_scalar(scale[:, i, :], src[:, 0:BATCH], nb[:, 0:1], 1.0, ALU.add, ALU.add)
                nc.vector.tensor_scalar(shift[:, i, :], src[:, BATCH:], nb[:, 1:2], None, ALU.add)
            dve.wait_ge(s_bias, 1)
            nc.vector.tensor_copy(mem["bias"][:], misc[0][:, 0:3 * D]).then_inc(s_mod, 1)
            dve.wait_ge(s_mod, 1)
            following.normalised(dve, 0, 0)
            following.statistics(dve, 1)
            low_parts(1, 0)
            following.modulate(dve, 0, 0)
            following.normalised(dve, 1, 1)
            low_parts(1, 1)

        @block.tensor
        def _(pe):
            pe.wait_ge(s_ident, 2)

            def turned(n):
                if n >= NR:
                    pe.wait_ge(s_free, n - NR + 1)
                if products_before(n - NR + 1):
                    pe.wait_ge(s_lo, products_before(n - NR + 1))
                return ring[n % NR]

            for a in range(2):
                n = a * TURNS
                for m in range(3):
                    pe.wait_ge(s_w[a][m], 16)
                    for c in range(TB):
                        bank = turned(n)
                        for i in range(PB):
                            k = PB * c + i
                            ins = nc.tensor.transpose(bank[:, P * i:P * i + P], w_in[a][m][:, P * k:P * k + P], ident[:])
                        ins.then_inc(s_full, 1)
                        n += 1
                if a == 1:
                    pe.wait_ge(s_cT, 1)
                    for i in range(3):
                        for c in range(2):
                            o = BATCH * (2 * i + c)
                            ins = nc.tensor.matmul(misc[1][:, o:o + BATCH], nw[:, i, D * c:D * c + D], rowsT[:, 0:BATCH],
                                                   start=True, stop=True)
                    ins.then_inc(s_emb, 1)
                    pe.wait_ge(s_ones, 1)
                    nc.tensor.matmul(misc[0][:, 0:3 * D], ones[:], biases[:].rearrange("a b d -> a (b d)"),
                                     start=True, stop=True).then_inc(s_bias, 1)
                pe.wait_ge(s_free, n)
                pe.wait_ge(s_w[a][3], 16)
                for product, (left, right) in enumerate(((wT[1], wT[0]), (wT[2], wo[a]))):
                    for i in range(AB):
                        par, c = i // (AB // 2), i % (AB // 2)
                        half = slice(dh * par, dh * par + dh)
                        bank = turned(n)
                        for j in range(PB):
                            k = PB * c + j
                            ins = nc.tensor.matmul(bank[:, D * j:D * j + D], left[half, k, :], right[half, k, :],
                                                   start=True, stop=True)
                        ins.then_inc(s_full, 1)
                        n += 1
                    if a == 1 and product == 0:
                        following.transpose_tokens(pe, 0, 0)
                if a == 0:
                    pe.wait_ge(s_cond0, 16)
                    pe.wait_ge(s_cond, 16 * 11)
                    nc.tensor.transpose(misc[0][:, 0:NROW], rows[:], ident[0:NROW, 0:NROW]).then_inc(s_rowsT, 1)


def feed_forward_phase(nc, sizes, mem, intake, ff, inputs, out):
    S, D, NG = sizes["S"], sizes["D"], sizes["NG"]
    E, F = sizes["E"], sizes["F"]
    DFF = sizes["DFF"]
    GT = 4 * S
    FB, EB = DFF // P, F // P
    y, ident = mem["y"], mem["ident"]

    with ExitStack() as ctx:
        def sb(n, shape, dt=F32):
            return ctx.enter_context(nc.sbuf_tensor(f"ff_{n}", shape, dt))

        def ps(n, shape):
            return ctx.enter_context(nc.psum_tensor(f"ff_{n}", shape, F32))

        def sem(n):
            return ctx.enter_context(nc.semaphore(f"ff_{n}"))

        e1_hi, e1_lo = (a.rearrange("d (e f) -> d e f", e=E) for a in (ff.e1_hi, ff.e1_lo))
        e2, routerT, x = ff.e2, mem["rowsT"][:, 0:E], ff.x
        iota = sb("iota", [P, E])
        euler = sb("euler", [P, 2])
        odd = sb("odd", [P, 2, D])
        xn = sb("xn", [P, 2, D])
        xT = [sb(f"xT{u}", [D, GT]) for u in range(2)]
        x_hi = [sb(f"x_hi{u}", [D, GT], F32R) for u in range(2)]
        x_lo = [sb(f"x_lo{u}", [D, GT], F32R) for u in range(2)]
        eh = [sb(f"eh{i}", [P, EB, GT]) for i in range(E)]
        xstats = sb("xstats", [P, 2, 6])
        xmv = sb("xmv", [P, 2, 2])
        xvar = sb("xvar", [P, 2])
        xrstd = sb("xrstd", [P, 2])
        logits = sb("logits", [P, 2, E])
        best = sb("best", [P, 2, 8])
        place = sb("place", [P, 2, 8], U32)
        placef = sb("placef", [P, 2, 2])
        diff = sb("diff", [P, 2])
        ratio = sb("ratio", [P, 2])
        denom = sb("denom", [P, 2])
        p1 = sb("p1", [P, 2])
        p2 = sb("p2", [P, 2])
        second = sb("second", [P, 2, E])
        mix = [sb(f"mix{u}", [P, 2, E]) for u in range(2)]

        xps = ps("xps", [P, BANK])
        hps = [ps(f"hps{i}", [P, BANK]) for i in range(2)]
        ops = [ps(f"ops{i}", [P, BANK]) for i in range(2)]
        OB = BANK // D
        HALVES = E // OB
        ADDS = 2 * E + 2

        s_const = sem("const")
        s_xy0 = sem("xy0")
        s_ff, s_xy = ff.s_ff, ff.s_xy
        s_xs = sem("xs")
        s_xa = sem("xa")
        s_xv = sem("xv")
        s_xr = sem("xr")
        s_xn = sem("xn")
        s_xps = sem("xps")
        s_xhi = sem("xhi")
        s_xT = sem("xT")
        s_lg = sem("lg")
        s_lgs = sem("lgs")
        s_best = sem("best")
        s_place = sem("place")
        s_ratio = sem("ratio")
        s_soft = sem("soft")
        s_mix = sem("mix")
        s_eh = sem("eh_psum")
        s_eg = sem("eh")
        s_eo = sem("eo")
        s_acc = sem("acc")
        s_out = [sem(f"out{u}") for u in range(2)]
        block = ctx.enter_context(nc.Block())

        def job_start(job):
            return job * OB + max(job - (2 * HALVES - 2), 0)

        def steps(eng, body):
            body(-1, 1)
            body(0, 0)
            with eng.Fori(0, NG - 5, 2) as i:
                body(i + 1, 1)
                body(i + 2, 0)
            for g in range(NG - 3, NG):
                body(g, g % 2)

        @block.sync
        def _(sp):
            def body(g, u):
                if isinstance(g, int) and g < 0:
                    return
                sp.wait_ge(s_acc, g * ADDS + ADDS)
                sp.dma_start(out[bass.ds(g * 2, 2)].rearrange("t p d -> p t d"), x[u][:]).then_inc(s_out[u], 16)
                if not (isinstance(g, int) and g >= NG - 2):
                    sp.wait_ge(s_out[u], landed(g, u))
                    ff.load_x(sp, g + 2, u)
            steps(sp, body)
            for u in range(2):
                sp.wait_ge(s_out[u], landed(NG - 2 + u, u))

        @block.gpsimd
        def _(pool):
            nc.gpsimd.iota(iota[:], [[1, E]], base=0, channel_multiplier=0,
                           allow_small_or_imprecise_dtypes=True).then_inc(s_const, 1)
            nc.gpsimd.memset(euler[:], 2.718281828459045).then_inc(s_const, 1)
            pool.wait_ge(s_const, 2)

            def body(g, u):
                if not (isinstance(g, int) and (g < 0 or g >= NG - 2)):
                    intake.rstd(pool, g + 2)
                if not (isinstance(g, int) and g >= NG - 1):
                    pool.wait_ge(s_xv, g + 2)
                    nc.gpsimd.tensor_tensor(xrstd[:], xvar[:], mem["neg_half"][:, 0:2], ALU.pow).then_inc(s_xr, 1)
                    pool.wait_ge(s_place, g + 2)
                    nc.gpsimd.tensor_tensor(ratio[:], euler[:], diff[:], ALU.pow).then_inc(s_ratio, 1)
            steps(pool, body)

        @block.scalar
        def _(act):
            def expert(g, e):
                act.wait_ge(s_eh, g * E + (e + 1))
                nc.scalar.activation(eh[e][:], hps[e % 2][:], ACT.Gelu).then_inc(s_eg, 1)

            def body(g, u):
                static = isinstance(g, int)
                ahead = not (static and g >= NG - 1)
                now = not (static and g < 0)
                for e in range(E):
                    if ahead and now and 2 <= e < 2 + FB:
                        ff.gates(act, g + 1, e - 2)
                    if now:
                        expert(g, e)
                if ahead:
                    act.wait_ge(s_xps, g + 2)
                    nc.scalar.copy(xT[1 - u][:], xps[:, 0:GT])
                    nc.scalar.copy(x_hi[1 - u][:], xps[:, 0:GT]).then_inc(s_xhi, 1)
            steps(act, body)

        @block.vector
        def _(dve):
            dve.wait_ge(s_const, 2)

            def sum_xy(k, u):
                dve.wait_ge(ff.s_x[u], landed(k, u))
                dve.wait_ge(intake.s_yb, k + 1)
                nc.vector.tensor_tensor(x[u][:], x[u][:], y[:, bass.ds(k * 2, 2), :], ALU.add).then_inc(s_xy0, 1)

            def after_feed_forward(k, u):
                dve.wait_ge(s_ff, k + 1)
                dve.wait_ge(s_xy0, k + 1)
                nc.vector.tensor_tensor(x[u][:], ff.banks[0][:, 0:2 * D].rearrange("p (t d) -> p t d", d=D), x[u][:],
                                        ALU.add).then_inc(s_xy, 1)
                dve.wait_ge(s_xy, k + 1)
                for t in range(2):
                    ins = nc.vector.bn_stats(xstats[:, t, :], x[u][:, t, :])
                ins.then_inc(s_xs, 1)
                dve.wait_ge(s_xs, 1)
                dve.wait_ge(s_xs, k + 1)
                for t in range(2):
                    ins = nc.vector.bn_aggr(xmv[:, t, :], xstats[:, t, :])
                ins.then_inc(s_xa, 1)
                dve.wait_ge(s_xa, k + 1)
                nc.vector.tensor_scalar(xvar[:], xmv[:, :, 1], EPS, None, ALU.add).then_inc(s_xv, 1)

            def normalised_x(k, u):
                dve.wait_ge(s_xr, k + 1)
                for t in range(2):
                    ins = nc.vector.tensor_scalar(xn[:, t, :], x[u][:, t, :], xmv[:, t, 0:1], xrstd[:, t:t + 1],
                                                  ALU.subtract, ALU.mult)
                ins.then_inc(s_xn, 1)

            def transposed_x(k, u):
                dve.wait_ge(s_xhi, k + 1)
                nc.vector.tensor_tensor(x_lo[u][:], xps[:, 0:GT], x_hi[u][:].bitcast(F32), ALU.subtract).then_inc(s_xT, 1)

            def route(k, u):
                dve.wait_ge(s_lg, k + 1)
                nc.vector.tensor_copy(logits[:], xps[:, GT:GT + 2 * E].rearrange("p (t e) -> p t e", e=E)).then_inc(s_lgs, 1)
                dve.wait_ge(s_lgs, 1)
                dve.wait_ge(s_lgs, k + 1)
                for t in range(2):
                    ins = nc.vector.max(best[:, t, :], logits[:, t, :])
                ins.then_inc(s_best, 1)
                dve.wait_ge(s_best, 1)
                dve.wait_ge(s_best, k + 1)
                for t in range(2):
                    nc.vector.max_index(place[:, t, :], best[:, t, :], logits[:, t, :])
                nc.vector.tensor_tensor(diff[:], best[:, :, 1], best[:, :, 0], ALU.subtract).then_inc(s_place, 1)

            def mixture(k, u):
                dve.wait_ge(s_place, k + 1)
                nc.vector.tensor_copy(placef[:], place[:, :, 0:2])
                dve.wait_ge(s_ratio, k + 1)
                nc.vector.tensor_scalar(denom[:], ratio[:], 1.0, None, ALU.add).then_inc(s_soft, 1)
                dve.wait_ge(s_soft, k * 4 + 1)
                nc.vector.reciprocal(p1[:], denom[:]).then_inc(s_soft, 1)
                dve.wait_ge(s_soft, k * 4 + 2)
                nc.vector.tensor_tensor(p2[:], p1[:], ratio[:], ALU.mult).then_inc(s_soft, 1)
                dve.wait_ge(s_soft, k * 4 + 3)
                for t in range(2):
                    ins = nc.vector.tensor_scalar(second[:, t, :], iota[:], placef[:, t, 1:2], p2[:, t:t + 1],
                                                  ALU.is_equal, ALU.mult)
                    ins = nc.vector.tensor_scalar(mix[u][:, t, :], iota[:], placef[:, t, 0:1], p1[:, t:t + 1],
                                                  ALU.is_equal, ALU.mult)
                ins.then_inc(s_soft, 1)
                dve.wait_ge(s_soft, k * 4 + 4)
                nc.vector.tensor_tensor(mix[u][:], mix[u][:], second[:], ALU.add).then_inc(s_mix, 1)

            def add_experts(g, u, job):
                half, t = job // 2, job % 2
                xt, ot = x[u][:, t, :], odd[:, t, :]
                dve.wait_ge(s_eo, g * 2 * HALVES + (job + 1))
                if job == 0:
                    dve.wait_ge(s_mix, g + 1)
                    if not (isinstance(g, int) and g == 0):
                        dve.wait_ge(s_acc, g * ADDS)
                for i in range(OB):
                    e = OB * half + i
                    if e >= 2:
                        before = job_start(2 * (half - 1) + t) + OB - 2 + i if i < 2 else job_start(job) + i - 2
                        dve.wait_ge(s_acc, g * ADDS + (before + 1))
                    src, w = ops[t][:, D * i:D * i + D], mix[u][:, t, e:e + 1]
                    if e == 1:
                        ins = nc.vector.tensor_scalar(ot, src, w, None, ALU.mult)
                    else:
                        to = ot if e % 2 else xt
                        ins = nc.vector.scalar_tensor_tensor(out=to, in0=src, scalar=w, in1=to, op0=ALU.mult, op1=ALU.add)
                    ins.then_inc(s_acc, 1)
                if half == HALVES - 1:
                    dve.wait_ge(s_acc, g * ADDS + (job_start(job) + OB))
                    nc.vector.tensor_tensor(xt, xt, ot, ALU.add).then_inc(s_acc, 1)

            def body(g, u):
                static = isinstance(g, int)
                now = not (static and g < 0)
                ahead = not (static and g >= NG - 1)
                stats_ahead = not (static and (g < 0 or g >= NG - 2))
                if ahead and now:
                    ff.gated(dve, g + 1, 0)
                if stats_ahead:
                    intake.statistics(dve, g + 2)
                if ahead and now:
                    for c in range(1, FB):
                        ff.gated(dve, g + 1, c)
                if now:
                    mixture(g, u)
                if ahead:
                    sum_xy(g + 1, 1 - u)
                if stats_ahead:
                    intake.normalised(dve, g + 2, u)
                if ahead:
                    after_feed_forward(g + 1, 1 - u)
                if now:
                    add_experts(g, u, 0)
                if ahead:
                    normalised_x(g + 1, 1 - u)
                if now:
                    add_experts(g, u, 1)
                if not (static and g >= NG - 2):
                    intake.modulate(dve, g + 2, u)
                if ahead:
                    transposed_x(g + 1, 1 - u)
                if now:
                    add_experts(g, u, 2)
                if ahead:
                    route(g + 1, 1 - u)
                if now:
                    add_experts(g, u, 3)
            steps(dve, body)

        @block.tensor
        def _(pe):
            def transpose_x(k, u):
                pe.wait_ge(s_xn, k + 1)
                for t in range(2):
                    ins = nc.tensor.transpose(xps[:, P * t:P * t + P], xn[:, t, :], ident[:])
                ins.then_inc(s_xps, 1)

            def router_logits(k, u):
                pe.wait_ge(s_xT, k + 1)
                for t in range(2):
                    ins = nc.tensor.matmul(xps[:, GT + E * t:GT + E * t + E], xT[u][:, P * t:P * t + P], routerT,
                                           start=True, stop=True)
                ins.then_inc(s_lg, 1)

            def expert_hidden(g, u, e):
                if not (isinstance(g, int) and g == 0 and e < 2):
                    pe.wait_ge(s_eg, g * E + (e - 1))
                for c in range(EB):
                    o = hps[e % 2][:, GT * c:GT * c + GT]
                    nc.tensor.matmul(o, e1_hi[:, e, P * c:P * c + P], x_hi[u][:], start=True, stop=False)
                    nc.tensor.matmul(o, e1_hi[:, e, P * c:P * c + P], x_lo[u][:], start=False, stop=False)
                    ins = nc.tensor.matmul(o, e1_lo[:, e, P * c:P * c + P], x_hi[u][:], start=False, stop=True)
                ins.then_inc(s_eh, 1)

            def expert_out(g, job):
                half, t = job // 2, job % 2
                if half:
                    pe.wait_ge(s_acc, g * ADDS + (job_start(t) + OB))
                elif not (isinstance(g, int) and g == 0):
                    pe.wait_ge(s_acc, g * ADDS + (job_start(2 * HALVES - 2 + t) + OB - ADDS))
                for i in range(OB):
                    e = OB * half + i
                    if t == 0:
                        pe.wait_ge(s_eg, g * E + (e + 1))
                    for c in range(EB):
                        ins = nc.tensor.matmul(ops[t][:, D * i:D * i + D], eh[e][:, c, P * t:P * t + P], e2[:, e, c, :],
                                               start=c == 0, stop=c == EB - 1)
                ins.then_inc(s_eo, 1)

            def body(g, u):
                static = isinstance(g, int)
                now = not (static and g < 0)
                ahead = not (static and g >= NG - 1)
                for e in range(E - 1):
                    if ahead and now and 2 <= e < 2 + FB:
                        ff.hidden(pe, g + 1, 1 - u, e - 2)
                    if now:
                        expert_hidden(g, u, e)
                if ahead and now:
                    ff.output(pe, g + 1)
                if now:
                    expert_hidden(g, u, E - 1)
                    expert_out(g, 0)
                if not (static and g >= NG - 2):
                    intake.transpose_tokens(pe, g + 2, u)
                if now:
                    expert_out(g, 1)
                if ahead:
                    transpose_x(g + 1, 1 - u)
                if now:
                    expert_out(g, 2)
                    expert_out(g, 3)
                if ahead:
                    router_logits(g + 1, 1 - u)
            steps(pe, body)


def build(nc, inputs, out):
    BATCH, S, D = inputs["x"].shape
    INNER = inputs["attn1_wq"].shape[1]
    E, _, F = inputs["e_w1"].shape
    T = BATCH * S
    sizes = dict(S=S, D=D, BATCH=BATCH, H=INNER // 64, NG=T // (4 * S), E=E, F=F, DFF=inputs["ff_w2"].shape[0])
    inputs = dict(inputs)
    tiles = "(t two) s d -> t (two s) d"
    inputs["x"] = inputs["x"].rearrange(tiles, two=2)
    context = inputs["context"].rearrange(tiles, two=2)
    out = out.rearrange(tiles, two=2)
    H, NT, GT = sizes["H"], T // P, 4 * S

    with ExitStack() as ctx:
        def sb(n, shape, dt=F32):
            return ctx.enter_context(nc.sbuf_tensor(n, shape, dt))

        mem = dict(
            y=sb("y", [P, NT, D]),
            scale=sb("scale", [D, 3, BATCH]),
            shift=sb("shift", [D, 3, BATCH]),
            rowsT=sb("rowsT", [D, sizes["E"] + 2 * sizes["DFF"] // P]),
            bias=sb("bias", [P, 3 * D]),
            ident=sb("ident", [P, P]),
            neg_half=sb("neg_half", [P, NT]),
            z=[sb(f"z{u}", [P, 2, D]) for u in range(2)],
            hT=[sb(f"hT{u}", [D, GT]) for u in range(2)],
            c_in=[sb(f"c_in{u}", [P, 2, D]) for u in range(2)],
            sT=[sb(f"sT{u}", [D, GT]) for u in range(2)],
            s_hi=[sb(f"s_hi{u}", [D, GT], F32R) for u in range(2)],
            s_lo=[sb(f"s_lo{u}", [D, GT], F32R) for u in range(2)],
            w_hi=[sb(f"w_hi{u}", [D, 2, 2, S], F32R) for u in range(2)],
            w_lo=[sb(f"w_lo{u}", [D, 2, 2, S], F32R) for u in range(2)],
            stats=sb("stats", [P, 2, 6]),
            mv=sb("mv", [P, 2, 2]),
            var=sb("var", [P, 2]),
            rstd=sb("rstd", [P, 2]),
            two_banks=ctx.enter_context(nc.psum_tensor("two_banks", [P, 2 * BANK], F32)),
            tps=ctx.enter_context(nc.psum_tensor("tps", [P, BANK], F32)),
        )
        intake1 = Intake(nc, ctx, "in1", sizes, mem, 0, mem["bias"][:, 0:D], None)
        intake2 = Intake(nc, ctx, "in2", sizes, mem, 1, mem["bias"][:, D:2 * D], intake1, context)
        intake3 = Intake(nc, ctx, "in3", sizes, mem, 2, mem["bias"][:, 2 * D:3 * D], intake2, swaps=False)

        def products(a):
            return [sb(f"{n}{a}", shape, F32R)
                    for n, shape in (("A_hi", [D, H, D]), ("A_lo", [D, H, D]), ("B_hi", [D, 2, H // 2, D]),
                                     ("B_lo", [D, 2, H // 2, D]))]

        mem["attn"] = [products(a) for a in range(2)]
        setup_phase(nc, sizes, mem, inputs, intake1)

        ff = FeedForward(nc, ctx, sizes, mem, inputs, intake3)
        attention_phase(nc, sizes, mem, [intake1, intake2, intake3], mem["attn"], ff)
        feed_forward_phase(nc, sizes, mem, intake3, ff, inputs, out)


_INS = ["x", "cond_1024", "ctx_1024"] + [f"L0_xcond_{n}" for n in (
    "attn1_wq", "attn1_wk", "attn1_wv", "attn1_wo", "attn1_bo", "attn2_wq", "attn2_wk", "attn2_wv", "attn2_wo",
    "attn2_bo", "ff_w1", "ff_b1", "ff_w2", "ff_b2", "norm1_w", "norm1_b", "norm2_w", "norm2_b", "norm3_w",
    "norm3_b")] + ["L0_ffn_router_w", "L0_ffn_w1", "L0_ffn_w2"]
_NAMES = {"cond_1024": "cond", "ctx_1024": "context", "L0_ffn_router_w": "router_w", "L0_ffn_w1": "e_w1",
          "L0_ffn_w2": "e_w2"}


def kernel(**inputs):
    import numpy as _np
    import concourse.bacc as _bacc
    from concourse import mybir as _mybir
    from concourse.bass_utils import run_bass_kernel_spmd as _run

    nc = _bacc.Bacc("TRN2", target_bir_lowering=False, num_devices=1)
    arrays, aps = {}, {}
    for name in _INS:
        a = _np.ascontiguousarray(inputs[name])
        arrays[f"in_{name}"] = a
        short = _NAMES.get(name, name.replace("L0_xcond_", ""))
        aps[short] = nc.dram_tensor(f"in_{name}", a.shape, _mybir.dt.from_np(a.dtype), kind="ExternalInput").ap()
    out = nc.dram_tensor("out", inputs["x"].shape, F32, kind="ExternalOutput").ap()
    build(nc, aps, out)
    r = _run(nc, [arrays], core_ids=[0])
    return r.results[0]["out"]
```
